# Optimizing a Trainium2 kernel written in Bass

```python
import numpy as np
import jax
import jax.numpy as jnp

def _softmax(x, axis=-1):
    return jax.nn.softmax(x, axis=axis)

def _gelu(x):
    return jax.nn.gelu(x, approximate=True)

def _silu(x):
    return jax.nn.silu(x)

def _sigmoid(x):
    return jax.nn.sigmoid(x)

def _layernorm(x, axis=-1, eps=1e-05):
    m = jnp.mean(x, axis=axis, keepdims=True)
    v = jnp.var(x, axis=axis, keepdims=True)
    return (x - m) / jnp.sqrt(v + eps)

def _scatter_add(tgt, idx, src, axis=0):
    return tgt.at[idx].add(src)

def _segment_sum(src, seg, n):
    return jax.ops.segment_sum(src, seg, n)
kernel_name = 'mk_xattn_ffn_d1_seqx_r4_818720'

def setup_inputs(seed: int=0):
    np.random.seed(seed)
    _w = jnp.asarray

    def _rec_inputs():
        import jax
        import jax.numpy as jnp
        _rk = jax.random.key(seed)
        x = -0.0003929 + 0.9999 * jax.random.normal(jax.random.fold_in(_rk, 1), (16, 128, 1024), jnp.float32)
        _lenS = 128 - jax.random.randint(jax.random.fold_in(_rk, 7), (16,), 0, max(1, 128 // 4) + 1, jnp.int32)
        _lenS2 = 128 - jax.random.randint(jax.random.fold_in(_rk, 8), (16,), 0, max(1, 128 // 4) + 1, jnp.int32)
        _ctx_4096P = jax.random.normal(jax.random.fold_in(_rk, 11), (16, 16, 1024), jnp.float32)
        _ctx_4096c = jax.random.dirichlet(jax.random.fold_in(_rk, 511), 0.3 * jnp.ones((16,), jnp.float32), (16, 128))
        _ctx_4096t = jnp.einsum('bsk,bkd->bsd', _ctx_4096c, _ctx_4096P)
        _ctx_4096t = _ctx_4096t * jax.lax.rsqrt(jnp.mean(jnp.square(_ctx_4096t)) + 1e-12) * 0.953939
        ctx_4096 = 2.81802e-05 + 1.00001 * (_ctx_4096t + 0.3 * jax.random.normal(jax.random.fold_in(_rk, 611), (16, 128, 1024), jnp.float32))
        _validS = jnp.arange(128)[None, :] < _lenS[:, None]
        _validS2 = jnp.arange(128)[None, :] < _lenS2[:, None]
        _causal = jnp.tril(jnp.ones((128, 128), dtype=bool))
        mask_SxS2_bk0 = jnp.logical_not(jnp.broadcast_to(_validS2[0:1, :], (128, 128)))
        return (x, ctx_4096, mask_SxS2_bk0)
    x, ctx_4096, mask_SxS2_bk0 = _rec_inputs()

    def _L0_xattn_setup():
        import jax, jax.numpy as jnp
        import numpy as np
        N_HEAD = 32
        D_MODEL = 1024
        N_KV_GROUPS = 8
        D_HEAD = D_MODEL // N_HEAD
        H_PER_G = N_HEAD // N_KV_GROUPS
        KV_DIM = N_KV_GROUPS * D_HEAD
        B, S = (2, 512)
        key = jax.random.key(seed)
        ks = jax.random.split(key, 8)
        q = jax.random.normal(ks[0], (B, S, D_MODEL), dtype=jnp.float32)
        k = jax.random.normal(ks[1], (B, S, D_MODEL), dtype=jnp.float32)
        v = jax.random.normal(ks[2], (B, S, D_MODEL), dtype=jnp.float32)
        mask = jnp.tril(jnp.ones((S, S), dtype=bool))
        w_q = jax.random.uniform(ks[3], (D_MODEL, D_MODEL), dtype=jnp.float32) * 0.02
        w_k = jax.random.uniform(ks[4], (KV_DIM, D_MODEL), dtype=jnp.float32) * 0.02
        w_v = jax.random.uniform(ks[5], (KV_DIM, D_MODEL), dtype=jnp.float32) * 0.02
        w_out = jax.random.uniform(ks[6], (D_MODEL, D_MODEL), dtype=jnp.float32) * 0.02
        return {'q': q, 'k': k, 'v': v, 'w_q': w_q, 'w_k': w_k, 'w_v': w_v, 'w_out': w_out, 'mask': mask}
    _L0_xattn_all = _L0_xattn_setup()
    _L0_xattn_in = {k: v for k, v in _L0_xattn_all.items() if k in ('w_q', 'w_k', 'w_v', 'w_out')}
    del _L0_xattn_all

    def _L0_ffn_setup():
        import jax, jax.numpy as jnp
        import numpy as np
        M = 1024
        K = 1024

        def _make_2to4_mask(key, shape):
            scores = jax.random.normal(key, shape)
            g = scores.reshape(shape[0], shape[1] // 4, 4)
            rank = jnp.argsort(jnp.argsort(-jnp.abs(g), axis=-1), axis=-1)
            return (rank < 2).reshape(shape).astype(jnp.float32)
        key = jax.random.key(seed)
        k_x, k_w12, k_b12, k_w3, k_b3, k_m = jax.random.split(key, 6)
        x = jax.random.normal(k_x, (4, 512, K), dtype=jnp.float32)
        w12_dense = jax.random.normal(k_w12, (2 * M, K), dtype=jnp.float32) * (1.0 / np.sqrt(K))
        mask12 = _make_2to4_mask(k_m, (2 * M, K))
        w12 = w12_dense * mask12
        b12 = jax.random.normal(k_b12, (2 * M,), dtype=jnp.float32) * 0.01
        w3 = jax.random.normal(k_w3, (M, M), dtype=jnp.float32) * (1.0 / np.sqrt(M))
        b3 = jax.random.normal(k_b3, (M,), dtype=jnp.float32) * 0.01
        return {'x': x, 'w12': w12, 'b12': b12, 'w3': w3, 'b3': b3}
    _L0_ffn_all = _L0_ffn_setup()
    _L0_ffn_in = {k: v for k, v in _L0_ffn_all.items() if k in ('w12', 'b12', 'w3', 'b3')}
    del _L0_ffn_all
    return {'x': x, 'ctx_4096': ctx_4096, 'mask_SxS2_bk0': mask_SxS2_bk0, 'L0_xattn_w_q': _L0_xattn_in['w_q'], 'L0_xattn_w_k': _L0_xattn_in['w_k'], 'L0_xattn_w_v': _L0_xattn_in['w_v'], 'L0_xattn_w_out': _L0_xattn_in['w_out'], 'L0_ffn_w12': _L0_ffn_in['w12'], 'L0_ffn_b12': _L0_ffn_in['b12'], 'L0_ffn_w3': _L0_ffn_in['w3'], 'L0_ffn_b3': _L0_ffn_in['b3']}

def reference(x, ctx_4096, mask_SxS2_bk0, L0_xattn_w_q, L0_xattn_w_k, L0_xattn_w_v, L0_xattn_w_out, L0_ffn_w12, L0_ffn_b12, L0_ffn_w3, L0_ffn_b3):
    import jax
    import jax.numpy as jnp

    def _L0_xattn_ref(q, k, v, w_q, w_k, w_v, w_out, mask):
        import jax, jax.numpy as jnp
        import numpy as np
        N_HEAD = 32
        D_MODEL = 1024
        N_KV_GROUPS = 8
        D_HEAD = D_MODEL // N_HEAD
        H_PER_G = N_HEAD // N_KV_GROUPS
        KV_DIM = N_KV_GROUPS * D_HEAD
        B, S = (2, 512)
        b, n, _ = q.shape
        s = k.shape[1]
        query = q @ w_q.T
        key = k @ w_k.T
        value = v @ w_v.T
        query = query.reshape(b, n, N_HEAD, D_HEAD).transpose(0, 2, 1, 3)
        query = query.reshape(b, N_KV_GROUPS, H_PER_G, n, D_HEAD)
        key = key.reshape(b, s, N_KV_GROUPS, D_HEAD).transpose(0, 2, 1, 3)
        value = value.reshape(b, s, N_KV_GROUPS, D_HEAD).transpose(0, 2, 1, 3)
        scores = jnp.einsum('bghnd,bgsd->bghns', query, key) / D_HEAD ** 0.5
        scores = jnp.where(mask, scores, jnp.finfo(scores.dtype).min)
        attention = jax.nn.softmax(scores, axis=-1)
        out = jnp.einsum('bghns,bgsd->bghnd', attention, value)
        out = out.transpose(0, 3, 1, 2, 4).reshape(b, n, D_MODEL)
        return out @ w_out.T

    def _L0_ffn_ref(x, w12, b12, w3, b3):
        import jax, jax.numpy as jnp
        import numpy as np
        M = 1024
        K = 1024

        def _make_2to4_mask(key, shape):
            scores = jax.random.normal(key, shape)
            g = scores.reshape(shape[0], shape[1] // 4, 4)
            rank = jnp.argsort(jnp.argsort(-jnp.abs(g), axis=-1), axis=-1)
            return (rank < 2).reshape(shape).astype(jnp.float32)
        x12 = jnp.einsum('bsk,mk->bsm', x, w12) + b12
        x1, x2 = jnp.split(x12, 2, axis=-1)
        x4 = jax.nn.silu(x1) * x2
        return jnp.einsum('bsm,nm->bsn', x4, w3) + b3
    x = x + _L0_xattn_ref(_layernorm(x, axis=-1), ctx_4096, ctx_4096, L0_xattn_w_q, L0_xattn_w_k, L0_xattn_w_v, L0_xattn_w_out, mask_SxS2_bk0)
    x = x + _L0_ffn_ref(_layernorm(x, axis=-1), L0_ffn_w12, L0_ffn_b12, L0_ffn_w3, L0_ffn_b3)
    return x

_drawn_inputs = setup_inputs


def setup_inputs(seed=0):
    import zlib

    import numpy as np

    out = dict(_drawn_inputs(seed))
    spreads = {}
    factors = {'L0_xattn_w_out': 2.855, 'L0_ffn_b12': 30.053, 'L0_ffn_b3': 21.992}
    for name, (base, spread) in spreads.items():
        noise = np.random.default_rng([zlib.crc32(name.encode()), seed]).standard_normal(out[name].shape)
        drawn = base * np.exp(spread * noise) if base else spread * noise
        out[name] = jnp.asarray(drawn.astype(out[name].dtype))
    for name, factor in factors.items():
        out[name] = (out[name] * factor).astype(out[name].dtype)
    return out
```

```python
from contextlib import ExitStack

import concourse.bass as bass
from concourse import mybir

F32 = mybir.dt.float32
F16 = mybir.dt.float16
U32 = mybir.dt.uint32
U8 = mybir.dt.uint8
ALU = mybir.AluOpType
ACT = mybir.ActivationFunctionType
AX_X = mybir.AxisListType.X
RMAX = bass.bass_isa.ReduceOp.max

P = 128
D = 1024
KC = D // P
SEQ = 128
HEADS, GROUPS, DH = 32, 8, 32
HPG = HEADS // GROUPS
KV = GROUPS * DH
TOK = 16 * SEQ
U = 2
AB = U * SEQ
NB = TOK // AB
FB = 512
NF = TOK // FB
FT = FB // P
M = D
MC = M // P
HALF = 512
EPS = 1e-5
VW = DH + 2
EXPONENT = 0x7F800000
MASKED = -(2.0 ** 100)
XN_SCALE = 2.0 ** 8
W_SCALE = 2.0 ** 13
Q_FACTOR = 2.0 ** -15 * DH ** -0.5
KV_FACTOR = 2.0 ** -23
C_SCORE = 2.0 ** -9
C_OUT = 2.0 ** -16
C_HID = 2.0 ** -21
C_FFN = 2.0 ** -26
NDMA_STACK = 12


def xattn_ffn(nc, x, ctx_t, mask, wq_t, wk_t, wv_t, wo_t, w12_t, b12_t, w3_t, b3_row, out):
    x_blocks = x.rearrange("(b u p) d -> b p u d", b=NB, p=P)
    x1_dram = nc.dram_tensor("x1_scratch", (TOK, D), F32, kind="Internal").ap()
    x1_blocks = x1_dram.rearrange("(b u p) d -> b p u d", b=NB, p=P)
    x1_ffn = x1_dram.rearrange("(b u p) d -> b p u d", b=NF, p=P)
    out_ffn = out.rearrange("(b u p) d -> b p u d", b=NF, p=P)

    def at(blocks, i):
        return blocks[bass.ds(i, 1)].rearrange("o p u d -> (o p) u d")

    with ExitStack() as stack:
        def sb(name, shape, dt):
            return stack.enter_context(nc.sbuf_tensor(name, shape, dt))

        def sem(name):
            return stack.enter_context(nc.semaphore(name))

        arena_in = sb("arena_in", [P, 32768], F16)
        arena_out = sb("arena_out", [P, 16384], F16)
        arena_work = sb("arena_work", [P, 32768], F16)
        wstage = sb("wstage", [P, 4096], F32)

        def carve(arena, at_, n, dt=F16):
            w = n * (2 if dt is F32 else 1)
            v = arena[:, at_:at_ + w]
            return (v.bitcast(dt) if dt is F32 else v), at_ + w

        o = 0
        wq, o = carve(arena_in, o, 2 * GROUPS * KC * P)
        wq = wq.rearrange("p (s m c o) -> p s m c o", s=2, m=GROUPS, c=KC)
        wk, o = carve(arena_in, o, 2 * KC * KV)
        wk = wk.rearrange("p (s c o) -> p s c o", s=2, c=KC)
        wv, o = carve(arena_in, o, 2 * KC * KV)
        wv = wv.rearrange("p (s c o) -> p s c o", s=2, c=KC)
        ctx_in, o = carve(arena_in, o, KC * AB, F32)
        ctx, o = carve(arena_in, o, 2 * KC * AB)
        ctx = ctx.rearrange("p (s c n) -> p s c n", s=2, c=KC)
        wo = arena_out[:, :].rearrange("p (h s c o) -> p h s c o", h=2, s=2, c=KC)
        w12 = arena_in[:, :].rearrange("p (m s c o) -> p m s c o", m=MC, s=2, c=KC)
        w3 = wo

        o = 0
        x_in, o = carve(arena_work, o, U * D, F32)
        x_in = x_in.rearrange("p (u d) -> p u d", u=U)
        x_res, o = carve(arena_work, o, U * D, F32)
        x_res = x_res.rearrange("p (u d) -> p u d", u=U)
        xn, o = carve(arena_work, o, 2 * KC * AB)
        xn = xn.rearrange("p (s c n) -> p s c n", s=2, c=KC)
        q_part, o = carve(arena_work, o, 2 * 2 * 2 * AB)
        q_part = q_part.rearrange("p (r s g n) -> p r s g n", r=2, s=2, g=2)
        q_stack, o = carve(arena_work, o, HEADS * AB)
        q_stack = q_stack.rearrange("p (g j n) -> p g j n", g=GROUPS, j=HPG)
        k_part, o = carve(arena_work, o, 2 * 2 * AB)
        k_part = k_part.rearrange("p (s b n) -> p s b n", s=2, b=2)
        k_stack, o = carve(arena_work, o, GROUPS * AB)
        k_stack = k_stack.rearrange("p (b g n) -> p b g n", b=2, g=GROUPS // 2)
        v_aug, o = carve(arena_work, o, 2 * U * GROUPS * VW)
        v_aug = v_aug.rearrange("p (s u g w) -> p s u g w", s=2, u=U, g=GROUPS)
        attn_t, o = carve(arena_work, o, 2 * GROUPS * AB)
        attn_t = attn_t.rearrange("p (s g n) -> p s g n", s=2, g=GROUPS)
        assert o <= arena_work.shape[1], o
        score = sb("score", [P, 4, U, HPG * SEQ], F32)
        prob_t = sb("prob_t", [P, 2, 2, U, HPG * SEQ], F16)
        attn = sb("attn", [P, 2, U * HPG * DH], F32)

        o = 0
        y_in, o = carve(arena_work, o, FT * D, F32)
        y_in = y_in.rearrange("p (u d) -> p u d", u=FT)
        y_res, o = carve(arena_work, o, FT * D, F32)
        y_res = y_res.rearrange("p (u d) -> p u d", u=FT)
        yn, o = carve(arena_work, o, 2 * KC * FB)
        yn = yn.rearrange("p (s c n) -> p s c n", s=2, c=KC)
        hid, o = carve(arena_work, o, 2 * MC * FB)
        hid = hid.rearrange("p (s c n) -> p s c n", s=2, c=MC)
        assert o <= arena_work.shape[1], o
        silu = prob_t[:, :, :, :, :].rearrange("p a b c d -> p (a b c d)")[:, 0:2 * 2 * FB].bitcast(F32) \
            .rearrange("p (r n) -> p r n", r=2)
        gated = score[:, 0, :, :]
        b3_all = score[:, 2, :, :].rearrange("p u n -> p (u n)")

        ident = sb("ident", [P, P], F32)
        mask_u8 = sb("mask_u8", [P, SEQ], U8)
        mask_add = sb("mask_add", [P, SEQ], F32)
        b12 = sb("b12", [P, 2 * MC], F32)
        b2_scaled = sb("b2_scaled", [P, MC], F32)
        NW = GROUPS + 2 + 2 + MC + 2
        CH_Q, CH_K, CH_V, CH_O = 0, GROUPS, GROUPS + 1, GROUPS + 2
        CH_12, CH_3 = CH_O + 2, CH_O + 2 + MC
        w_max = sb("w_max", [P, NW], F32)
        w_top = sb("w_top", [P, NW], F32)
        w_exp = sb("w_exp", [P, NW], F32)
        w_inv = sb("w_inv", [P, NW], F32)
        w_scale = sb("w_scale", [P, NW], F32)
        ctx_max = sb("ctx_max", [P, 1], F32)
        ctx_top = sb("ctx_top", [P, 1], F32)
        ctx_exp = sb("ctx_exp", [P, 1], F32)
        ctx_inv = sb("ctx_inv", [P, 1], F32)
        ctx_scale = sb("ctx_scale", [P, 1], F32)
        score_base = sb("score_base", [P, GROUPS], F32)
        out_base = sb("out_base", [P, 2], F32)
        c_score = sb("c_score", [P, GROUPS], F32)
        c_neg = sb("c_neg", [P, GROUPS], F32)
        c_out = sb("c_out", [P, 2], F32)
        c_hid = sb("c_hid", [P, MC], F32)
        c_hid_inv = sb("c_hid_inv", [P, MC], F32)
        hid_scale = sb("hid_scale", [P, MC], F32)
        c_ffn = sb("c_ffn", [P, 2], F32)
        bound = sb("bound", [P, 8], F32)
        row_max = sb("row_max", [P, 4, U * HPG], F32)
        neg_max = sb("neg_max", [P, 4, U * HPG], F32)
        inv_sum = sb("inv_sum", [P, U * HPG], F32)
        stats = sb("stats", [P, 2, 6], F32)
        moments = sb("moments", [P, 2, 2], F32)
        var_scaled = sb("var_scaled", [P, 2], F32)
        rstd = sb("rstd", [P, 2], F32)
        minus_half = sb("minus_half", [P, 1], F32)

        bank = [stack.enter_context(nc.psum_tensor(f"bank{i}", [P, HALF], F32)) for i in range(8)]
        B_SCORE, B_TURN, B_AV, B_ATTN_T, B_DENSE = bank[0:2], bank[2:4], bank[4], bank[5], bank[6:8]
        B_FFN = bank[4:8]
        B_XT = bank[0:4]

        s_mask, s_b12, s_b3 = sem("mask_loaded"), sem("b12_loaded"), sem("b3_loaded")
        s_wload = [sem(f"weights_loaded_{i}") for i in range(5)]
        s_wmax, s_wtop, s_wscale = sem("w_max_done"), sem("w_top_done"), sem("w_scale_done")
        s_whi, s_wready = sem("w_hi_done"), sem("w_ready")
        s_ident, s_vinit, s_maskadd = sem("ident_done"), sem("v_init_done"), sem("mask_add_done")
        s_xload, s_ctxload, s_xres = sem("x_loaded"), sem("ctx_loaded"), sem("x_res_loaded")
        s_ctxmax, s_ctxtop, s_ctxscale, s_ctx = sem("ctx_max_done"), sem("ctx_top_done"), sem("ctx_scale_done"), sem("ctx_ready")
        s_ctxhi = sem("ctx_hi_done")
        s_norm, s_stat, s_var, s_rstd = sem("norm_done"), sem("stats_done"), sem("var_done"), sem("rstd_done")
        s_xt, s_xthi, s_xn = sem("x_turned"), sem("xn_hi_done"), sem("xn_ready")
        s_dense, s_dhi, s_dread = sem("dense_done"), sem("dense_hi_done"), sem("dense_read")
        s_qst = [sem("q_stack_loaded_0"), sem("q_stack_loaded_1")]
        s_kst = sem("k_stack_loaded")
        s_score, s_sread, s_neg, s_prob = sem("score_done"), sem("score_read"), sem("neg_max_done"), sem("prob_done")
        s_pt, s_pthi, s_ptread = sem("prob_turned"), sem("prob_t_hi_done"), sem("prob_t_ready")
        s_av, s_inv, s_avread = sem("av_done"), sem("inv_sum_done"), sem("attn_ready")
        s_ot, s_othi, s_otread = sem("attn_turned"), sem("attn_t_hi_done"), sem("attn_t_ready")
        s_c, s_x1 = sem("c_done"), sem("x1_stored")
        s_chain, s_alone = sem("vector_chain"), sem("waits_alone")
        s_const, s_const3 = sem("ffn_consts_done"), sem("ffn_out_consts_done")
        s_scales, s_ctxstep = sem("block_scales_done"), sem("ctx_step_done")
        s_bmax, s_btop = sem("b_max_done"), sem("b_top_done")
        s_yload, s_yres, s_yresb = sem("y_loaded"), sem("y_res_loaded"), sem("y_res_with_b3")
        s_yt, s_ythi, s_yn = sem("y_turned"), sem("yn_hi_done"), sem("yn_ready")
        s_h, s_silu, s_gated, s_hhi, s_hid = sem("h_done"), sem("silu_done"), sem("gated_done"), sem("hid_hi_done"), sem("hid_ready")
        s_y, s_yread, s_out = sem("y_done"), sem("ffn_bank_read"), sem("out_stored")

        block = stack.enter_context(nc.Block())

        def dense0(t):
            return 0 if isinstance(t, int) and t == 0 else 16 * t - 4

        STEPS = GROUPS + 4

        def alone(engine):
            engine.sem_inc(s_alone, 1)

        def parts(w):
            return w[:, 0], w[:, 1]

        chunks = []
        for m in range(GROUPS):
            chunks.append((CH_Q + m, wq_t[m], m % 4, 1, wq[:, 0, m], wq[:, 1, m]))
        chunks.append((CH_K, wk_t, 0, 2, wk[:, 0], wk[:, 1]))
        chunks.append((CH_V, wv_t, 2, 2, wv[:, 0], wv[:, 1]))
        for h in range(2):
            chunks.append((CH_O + h, wo_t[h], 0, 4, wo[:, h, 0], wo[:, h, 1]))
        for m in range(MC):
            chunks.append((CH_12 + m, w12_t[m], 2 * (m % 2), 2, w12[:, m, 0], w12[:, m, 1]))
        for h in range(2):
            chunks.append((CH_3 + h, w3_t[h], 4 * h, 4, w3[:, h, 0], w3[:, h, 1]))
        last_user, w_arrival, loads = [None] * 8, [], [0] * 8
        for n, (_, _, slot, width, _, _) in enumerate(chunks):
            free_after = [last_user[s] for s in range(slot, slot + width) if last_user[s] is not None]
            for s in range(slot, slot + width):
                last_user[s] = n
            loads[slot] += 16
            w_arrival.append((max(free_after) + 1 if free_after else 0, loads[slot]))

        def stage(n):
            _, _, slot, width, _, _ = chunks[n]
            if slot == 4:
                return hid.rearrange("p s c n -> p (s c n)").bitcast(F32)
            return wstage[:, slot * 1024:(slot + width) * 1024]

        @block.sync
        def _(sp):
            def load_chunk(n):
                if w_arrival[n][0]:
                    sp.wait_ge(s_wready, w_arrival[n][0])
                sp.dma_start(stage(n), chunks[n][1]).then_inc(s_wload[chunks[n][2]], 16)

            def load_ctx(t):
                sp.dma_start(ctx_in[:, :], ctx_t[bass.ds(t, 1)].rearrange("o p n -> (o p) n")).then_inc(s_ctxload, 16)

            def stack_q(t, pair):
                sp.wait_ge(s_dread, dense0(t) + 2 * pair + 2)
                for j in range(HPG):
                    for r, part in ((0, 0), (1, 1), (2, 0)):
                        sp.dma_start(q_stack[DH * r:DH * r + DH, 2 * pair:2 * pair + 2, j, :],
                                     q_part[DH * j:DH * j + DH, pair % 2, part]).then_inc(s_qst[pair % 2], 16)

            def stack_k(t):
                sp.wait_ge(s_dread, dense0(t) + GROUPS + 2)
                for g in range(4):
                    for r, part in ((0, 0), (1, 0), (2, 1)):
                        sp.dma_start(k_stack[DH * r:DH * r + DH, :, g, :],
                                     k_part[DH * g:DH * g + DH, part]).then_inc(s_kst, 16)

            def load_x(t):
                sp.wait_ge(s_xt, 4 * t)
                alone(sp)
                sp.dma_start(x_in, at(x_blocks, t % NB)).then_inc(s_xload, 16)

            def iteration(t, project, attend):
                if project:
                    load_ctx(t)
                    load_x(t + 1)
                    for pair in range(GROUPS // 2):
                        if attend:
                            sp.wait_ge(s_score, 16 * (t - 1) + 4 * pair + 4)
                            alone(sp)
                        stack_q(t, pair)
                    if attend:
                        sp.wait_ge(s_score, 16 * t)
                        alone(sp)
                    stack_k(t)
                if attend:
                    sp.wait_ge(s_dread, dense0(t) + (16 if project else 4))
                    alone(sp)
                    sp.dma_start(at(x1_blocks, t - 1), x_res).then_inc(s_x1, 16)
                    if project:
                        sp.wait_ge(s_x1, 16 * t)
                        alone(sp)
                        sp.dma_start(x_res, at(x_blocks, t)).then_inc(s_xres, 16)

            sp.dma_start(x_in, at(x_blocks, 0)).then_inc(s_xload, 16)
            for n in range(2):
                load_chunk(n)
            sp.dma_start(mask_u8[:, :], mask).then_inc(s_mask, 16)
            for n in range(2, 6):
                load_chunk(n)
            load_ctx(0)
            stack_q(0, 0)
            for n in range(6, 8):
                load_chunk(n)
            load_x(1)
            stack_q(0, 1)
            for n in range(8, CH_O):
                load_chunk(n)
            stack_q(0, 2)
            sp.dma_start(x_res, at(x_blocks, 0)).then_inc(s_xres, 16)
            sp.dma_start(b12[:, :], b12_t).then_inc(s_b12, 16)
            stack_q(0, 3)
            load_chunk(CH_O)
            stack_k(0)
            load_chunk(CH_O + 1)
            with sp.Fori(1, NB) as t:
                sp.wait_ge(s_ctx, t)
                alone(sp)
                iteration(t, True, True)

            for n in range(CH_12, CH_3):
                load_chunk(n)
            iteration(NB, False, True)
            sp.wait_ge(s_x1, 16 * NB)
            sp.dma_start(y_in, at(x1_ffn, 0)).then_inc(s_yload, 16)
            for n in range(CH_3, NW):
                load_chunk(n)
            sp.dma_start(b3_all, b3_row.broadcast_to([P, D])).then_inc(s_b3, 16)
            sp.dma_start(y_res, at(x1_ffn, 0)).then_inc(s_yres, 16)
            with sp.Fori(0, NF) as f:
                sp.wait_ge(s_yt, 8 * f + 8)
                alone(sp)
                sp.dma_start(y_in, at(x1_ffn, (f + 1) % NF)).then_inc(s_yload, 16)
                for u in range(FT):
                    sp.wait_ge(s_yread, 8 * f + 2 * u + 10)
                    alone(sp)
                    sp.dma_start(at(out_ffn, f)[:, u], y_res[:, u]).then_inc(s_out, 16)
                sp.wait_ge(s_out, 16 * FT * (f + 1))
                alone(sp)
                sp.dma_start(y_res, at(x1_ffn, (f + 1) % NF)).then_inc(s_yres, 16)
            sp.wait_ge(s_yload, 16 * (NF + 1))
            sp.wait_ge(s_yres, 16 * (NF + 1))

        @block.gpsimd
        def _(pool):
            def top(n):
                pool.wait_ge(s_wmax, n + 1)
                pool.partition_all_reduce(w_top[:, chunks[n][0]:chunks[n][0] + 1],
                                          w_max[:, chunks[n][0]:chunks[n][0] + 1], P, RMAX).then_inc(s_wtop, 1)

            def root(n, r):
                pool.wait_ge(s_var, n + 1)
                pool.tensor_tensor(rstd[:, r:r + 1], var_scaled[:, r:r + 1], minus_half[:, :], ALU.pow)\
                    .then_inc(s_rstd, 1)

            def split_ctx(t):
                spread = ctx_scale[:, 0:1].broadcast_to([P, KC * AB])
                hi, lo = (ctx[:, s].rearrange("p c n -> p (c n)") for s in range(2))
                pool.wait_ge(s_ctxmax, t + 1)
                alone(pool)
                pool.partition_all_reduce(ctx_top[:, :], ctx_max[:, :], P, RMAX).then_inc(s_ctxtop, 1)
                pool.wait_ge(s_ctxscale, t + 1)
                if not (isinstance(t, int) and t == 0):
                    pool.wait_ge(s_dense, dense0(t))
                pool.tensor_tensor(hi, ctx_in[:, :], spread, ALU.mult).then_inc(s_ctxhi, 1)
                pool.wait_ge(s_ctxhi, 2 * t + 1)
                pool.tensor_tensor(ctx_in[:, :], ctx_in[:, :], spread, ALU.mult).then_inc(s_ctxhi, 1)
                pool.wait_ge(s_ctxhi, 2 * t + 2)
                pool.tensor_tensor(lo, ctx_in[:, :], hi, ALU.subtract).then_inc(s_ctx, 1)

            pool.memset(ident[:, :], 0.0).then_inc(s_ident, 1)
            pool.wait_ge(s_ident, 1)
            pool.affine_select(out=ident[:, :], in_=ident[:, :], compare_op=ALU.not_equal, fill=1.0, base=0,
                               pattern=[[-1, P]], channel_multiplier=1).then_inc(s_ident, 1)
            pool.memset(v_aug, 0.0).then_inc(s_vinit, 1)
            pool.memset(minus_half[:, :], -0.5).then_inc(s_vinit, 1)
            pool.wait_ge(s_vinit, 2)
            pool.memset(v_aug[:, 0, :, :, DH:DH + 1], 1.0).then_inc(s_vinit, 1)
            for u in range(U):
                root(u, u)
            for n in range(CH_O):
                top(n)
            split_ctx(0)
            for u in range(U):
                root(2 + u, u)
            for n in range(CH_O, CH_12):
                top(n)
            with pool.Fori(1, NB) as t:
                split_ctx(t)
                for u in range(U):
                    root(2 * t + 2 + u, u)
            for n in range(CH_12, CH_3):
                top(n)
            pool.wait_ge(s_bmax, 1)
            pool.partition_all_reduce(bound[:, 2:3], bound[:, 1:2], P, RMAX).then_inc(s_btop, 1)
            for u in range(FT):
                root(2 * (NB + 1) + u, u % 2)
            for n in range(CH_3, NW):
                top(n)
            pool.wait_ge(s_b3, 16)
            with pool.Fori(0, NF) as f:
                for u in range(FT):
                    root(2 * (NB + 1) + FT * (f + 1) + u, u % 2)
                pool.wait_ge(s_yres, 16 * f + 16)
                for u in range(FT):
                    ins = pool.tensor_tensor(y_res[:, u], y_res[:, u], b3_all, ALU.add)
                ins.then_inc(s_yresb, 1)

        @block.scalar
        def _(act):
            def high(n):
                c, _, _, _, hi, _ = chunks[n]
                act.wait_ge(s_wscale, n + 1)
                if n == CH_12:
                    act.wait_ge(s_dense, dense0(NB))
                if n == CH_3:
                    act.wait_ge(s_dense, dense0(NB) + 4)
                act.activation(hi.rearrange("p c o -> p (c o)"), stage(n), ACT.Copy,
                               scale=w_scale[:, c:c + 1]).then_inc(s_whi, 1)

            def turned_hi(t):
                for q in range(4):
                    u, h = q // 2, q % 2
                    act.wait_ge(s_xt, 4 * t + q + 1)
                    if q == 0 and not (isinstance(t, int) and t == 0):
                        act.wait_ge(s_dense, dense0(t - 1) + GROUPS)
                    act.activation(xn[:, 0, 4 * h:4 * h + 4, P * u:P * u + P],
                                   B_XT[q][:, :].rearrange("p (c n) -> p c n", c=4), ACT.Copy).then_inc(s_xthi, 1)

            def q_hi(t, m):
                if m % 2 == 0:
                    if not (isinstance(t, int) and t == 0 and m < 4):
                        act.wait_ge(s_qst[(m // 2) % 2], 16 * NDMA_STACK * (2 * t + m // 4))
                act.wait_ge(s_dense, dense0(t) + m + 1)
                act.activation(q_part[:, (m // 2) % 2, 0, m % 2], B_DENSE[m % 2][:, 0:AB], ACT.Copy,
                               scale=Q_FACTOR).then_inc(s_dhi, 1)

            def k_hi(t, b):
                if b == 0 and not (isinstance(t, int) and t == 0):
                    act.wait_ge(s_kst, 16 * NDMA_STACK * t)
                act.wait_ge(s_dense, dense0(t) + GROUPS + b + 1)
                act.activation(k_part[:, 0, b], B_DENSE[b][:, 0:AB], ACT.Copy, scale=KV_FACTOR).then_inc(s_dhi, 1)

            def v_hi(t, u, attend):
                if u == 0 and attend:
                    act.wait_ge(s_av, 8 * t)
                act.wait_ge(s_dense, dense0(t) + GROUPS + 2 + u + 1)
                act.activation(v_aug[:, 0, u, :, 0:DH], B_DENSE[u][:, 0:KV].rearrange("p (g w) -> p g w", g=GROUPS),
                               ACT.Copy, scale=KV_FACTOR).then_inc(s_dhi, 1)

            def exps(a, m, u):
                act.wait_ge(s_neg, 8 * a + m + 1)
                for j in range(HPG):
                    s = score[:, m % 4, u, SEQ * j:SEQ * j + SEQ]
                    ins = act.activation(s, s, ACT.Exp, bias=neg_max[:, m % 4, HPG * u + j:HPG * u + j + 1],
                                         scale=c_score[:, m:m + 1])
                ins.then_inc(s_prob, 1)

            def prob_hi(a, m):
                for u in range(U):
                    if u == 0 and m >= 2:
                        act.wait_ge(s_av, 8 * a + m - 1)
                    act.wait_ge(s_pt, 16 * a + 2 * m + u + 1)
                    act.activation(prob_t[:, m % 2, 0, u], B_TURN[u][:, :], ACT.Copy).then_inc(s_pthi, 1)

            def attn_hi(t, m):
                a = t - 1
                act.wait_ge(s_ot, 8 * a + m + 1)
                if m == 0:
                    act.wait_ge(s_dense, dense0(t))
                act.activation(attn_t[:, 0, m], B_ATTN_T[:, 0:AB], ACT.Copy).then_inc(s_othi, 1)

            def iteration(t, project, attend, chunk_at_step=None):
                a = t - 1
                for s in range(STEPS):
                    if chunk_at_step is not None and 1 <= s <= GROUPS:
                        high(chunk_at_step + s - 1)
                    if attend and 1 <= s <= GROUPS:
                        exps(a, s - 1, 0)
                    if attend and 2 <= s < GROUPS + 2:
                        prob_hi(a, s - 2)
                    if attend and 4 <= s:
                        attn_hi(t, s - 4)
                    if project and 1 <= s <= GROUPS:
                        q_hi(t, s - 1)
                    if attend and 1 <= s <= GROUPS:
                        exps(a, s - 1, 1)
                    if project and s in (GROUPS + 1, GROUPS + 2):
                        k_hi(t, s - GROUPS - 1)
                if project:
                    v_hi(t, 0, attend)
                    v_hi(t, 1, attend)
                    turned_hi(t + 1)

            high(0)
            turned_hi(0)
            high(1)
            for m in range(GROUPS):
                high(m + 2)
                q_hi(0, m)
            for b in range(2):
                k_hi(0, b)
            act.wait_ge(s_vinit, 3)
            for u in range(U):
                v_hi(0, u, False)
            turned_hi(1)
            for n in range(CH_O, CH_12):
                high(n)
            with act.Fori(1, NB) as t:
                iteration(t, True, True)
            iteration(NB, False, True, chunk_at_step=CH_12)

            def y_hi(f):
                for q in range(8):
                    act.wait_ge(s_yt, 8 * f + q + 1)
                    if q == 0 and not (isinstance(f, int) and f == 0):
                        act.wait_ge(s_h, 16 * f)
                    act.activation(yn[:, 0, 4 * (q % 2):4 * (q % 2) + 4, P * (q // 2):P * (q // 2) + P],
                                   B_XT[q % 4][:, :].rearrange("p (c n) -> p c n", c=4), ACT.Copy).then_inc(s_ythi, 1)

            y_hi(0)
            for n in range(CH_3, NW):
                high(n)
            act.wait_ge(s_const, 1)
            act.wait_ge(s_b12, 16)
            with act.Fori(0, NF) as f:
                for m in range(MC):
                    act.wait_ge(s_h, 16 * f + 2 * m + 1)
                    if m >= 2:
                        act.wait_ge(s_gated, 8 * f + m - 1)
                    act.activation(silu[:, m % 2], B_FFN[2 * (m % 2)][:, :], ACT.Silu, bias=b12[:, m:m + 1],
                                   scale=c_hid[:, m:m + 1]).then_inc(s_silu, 1)
                    act.wait_ge(s_gated, 8 * f + m + 1)
                    act.activation(hid[:, 0, m], gated[:, m % 2], ACT.Copy, scale=hid_scale[:, m:m + 1]).then_inc(s_hhi, 1)
                y_hi(f + 1)

        @block.tensor
        def _(pe):
            def product(dst, lhs, rhs):
                for c in range(KC):
                    for n, (a, b) in enumerate(((0, 0), (0, 1), (1, 0))):
                        ins = pe.matmul(dst, lhs(a, c), rhs(b, c), start=(c == 0 and n == 0),
                                        stop=(c == KC - 1 and n == 2))
                return ins

            def dense(t, k, dst, lhs, rhs):
                if not (isinstance(t, int) and t == 0 and k < 2):
                    pe.wait_ge(s_dread, dense0(t) + k - 1)
                product(dst, lhs, rhs).then_inc(s_dense, 1)

            def q_proj(t, m):
                if isinstance(t, int) and t == 0:
                    pe.wait_ge(s_wready, CH_Q + m + 1)
                if m == 0:
                    pe.wait_ge(s_xn, 4 * t + 4)
                dense(t, m, B_DENSE[m % 2][:, 0:AB], lambda s, c: wq[:, s, m, c], lambda s, c: xn[:, s, c])

            def k_proj(t, b):
                if b == 0:
                    pe.wait_ge(s_ctx, t + 1)
                dense(t, GROUPS + b, B_DENSE[b][:, 0:AB], lambda s, c: wk[:, s, c, P * b:P * b + P],
                      lambda s, c: ctx[:, s, c])

            def v_proj(t, u):
                dense(t, GROUPS + 2 + u, B_DENSE[u][:, 0:KV], lambda s, c: ctx[:, s, c, P * u:P * u + P],
                      lambda s, c: wv[:, s, c])

            def scores(t, m):
                a = t - 1
                if m == 0:
                    pe.wait_ge(s_kst, 16 * NDMA_STACK * t)
                    pe.wait_ge(s_xn, 4 * t + 4)
                if m % 2 == 0:
                    pe.wait_ge(s_qst[(m // 2) % 2], 16 * NDMA_STACK * (2 * a + m // 4 + 1))
                for u in range(U):
                    if m >= 1:
                        pe.wait_ge(s_sread, 16 * a + 2 * m + u - 1)
                    for j in range(HPG):
                        ins = pe.matmul(B_SCORE[u][:, SEQ * j:SEQ * j + SEQ],
                                        q_stack[0:3 * DH, m, j, SEQ * u:SEQ * u + SEQ],
                                        k_stack[0:3 * DH, m // 4, m % 4, SEQ * u:SEQ * u + SEQ], start=True, stop=True)
                    ins.then_inc(s_score, 1)

            def turn_prob(a, m):
                for u in range(U):
                    pe.wait_ge(s_prob, 16 * a + 2 * m + u + 1)
                    if m >= 1:
                        pe.wait_ge(s_ptread, 16 * a + 2 * m + u - 1)
                    for j in range(HPG):
                        ins = pe.transpose(B_TURN[u][:, SEQ * j:SEQ * j + SEQ],
                                           score[:, m % 4, u, SEQ * j:SEQ * j + SEQ], ident[:, :])
                    ins.then_inc(s_pt, 1)

            def weigh(t, m):
                a = t - 1
                if m == 0:
                    pe.wait_ge(s_dread, dense0(t))
                else:
                    pe.wait_ge(s_avread, 8 * a + m)
                pe.wait_ge(s_ptread, 16 * a + 2 * m + 2)
                for u in range(U):
                    for j in range(HPG):
                        dst = B_AV[:, VW * (HPG * u + j):VW * (HPG * u + j) + VW]
                        for n, (p, v) in enumerate(((0, 0), (0, 1), (1, 0))):
                            ins = pe.matmul(dst, prob_t[:, m % 2, p, u, SEQ * j:SEQ * j + SEQ], v_aug[:, v, u, m],
                                            start=(n == 0), stop=(n == 2))
                ins.then_inc(s_av, 1)

            def turn_attn(a, m):
                pe.wait_ge(s_avread, 8 * a + m + 1)
                if m >= 1:
                    pe.wait_ge(s_otread, 8 * a + m)
                for u in range(U):
                    ins = pe.transpose(B_ATTN_T[:, P * u:P * u + P], attn[:, m % 2, P * u:P * u + P], ident[:, :])
                ins.then_inc(s_ot, 1)

            def turn_x(t, attend):
                for q in range(4):
                    u, h = q // 2, q % 2
                    if h == 0:
                        pe.wait_ge(s_norm, 2 * t + u + 1)
                    if attend and q == 0:
                        pe.wait_ge(s_sread, 16 * (t - 1))
                    if attend and q == 2:
                        pe.wait_ge(s_ptread, 16 * (t - 1))
                    for c in range(4):
                        ins = pe.transpose(B_XT[q][:, P * c:P * c + P],
                                           x_in[:, u, P * (4 * h + c):P * (4 * h + c) + P], ident[:, :])
                    ins.then_inc(s_xt, 1)

            def out_proj(t, k0):
                a = t - 1
                for q in range(4):
                    u, h = q // 2, q % 2
                    if q == 0:
                        pe.wait_ge(s_otread, 8 * a + 8)
                    dense(t, k0 + q, B_DENSE[q % 2][:, :], lambda s, c: attn_t[:, s, c, P * u:P * u + P],
                          lambda s, c: wo[:, h, s, c])

            def iteration(t, project, attend):
                a = t - 1
                for s in range(STEPS):
                    if attend and s < GROUPS:
                        scores(t, s)
                    if attend and 2 <= s < GROUPS + 2:
                        turn_prob(a, s - 2)
                    if attend and 3 <= s < GROUPS + 3:
                        weigh(t, s - 3)
                    if attend and 4 <= s:
                        turn_attn(a, s - 4)
                    if project:
                        if s < GROUPS:
                            q_proj(t, s)
                        elif s < GROUPS + 2:
                            k_proj(t, s - GROUPS)
                        else:
                            v_proj(t, s - GROUPS - 2)
                if project:
                    turn_x(t + 1, attend)
                if attend:
                    out_proj(t, 12 if project else 0)

            pe.wait_ge(s_ident, 2)
            turn_x(0, False)
            pe.wait_ge(s_vinit, 3)
            for s in range(GROUPS):
                q_proj(0, s)
            pe.wait_ge(s_wready, CH_O)
            for b in range(2):
                k_proj(0, b)
            for u in range(U):
                v_proj(0, u)
            turn_x(1, False)
            pe.wait_ge(s_wready, CH_12)
            with pe.Fori(1, NB) as t:
                iteration(t, True, True)
            iteration(NB, False, True)

            def turn_y(f):
                for q in range(8):
                    u, h = q // 2, q % 2
                    if h == 0:
                        pe.wait_ge(s_norm, 2 * (NB + 1) + FT * f + u + 1)
                    if q >= 4:
                        pe.wait_ge(s_yn, 8 * f + q - 3)
                    for c in range(4):
                        ins = pe.transpose(B_XT[q % 4][:, P * c:P * c + P],
                                           y_in[:, u, P * (4 * h + c):P * (4 * h + c) + P], ident[:, :])
                    ins.then_inc(s_yt, 1)

            turn_y(0)
            with pe.Fori(0, NF) as f:
                pe.wait_ge(s_yn, 8 * f + 8)
                pe.wait_ge(s_wready, CH_3)
                for m in range(MC):
                    if m == 0:
                        pe.wait_ge(s_yread, 8 * f + 6)
                    elif m == 1:
                        pe.wait_ge(s_yread, 8 * f + 8)
                    else:
                        pe.wait_ge(s_gated, 8 * f + m - 1)
                    for k in range(2):
                        product(B_FFN[2 * (m % 2) + k][:, :], lambda s, c: w12[:, m, s, c, P * k:P * k + P],
                                lambda s, c: yn[:, s, c]).then_inc(s_h, 1)
                turn_y(f + 1)
                pe.wait_ge(s_wready, NW)
                pe.wait_ge(s_hid, 8 * f + 8)
                for q in range(8):
                    u, h = q // 2, q % 2
                    if q >= 4:
                        pe.wait_ge(s_yread, 8 * f + q + 5)
                    product(B_FFN[q % 4][:, :], lambda s, c: hid[:, s, c, P * u:P * u + P],
                            lambda s, c: w3[:, h, s, c]).then_inc(s_y, 1)

        @block.vector
        def _(dve):
            links = [0]

            def link(ins):
                ins.then_inc(s_chain, 1)
                links[0] += 1
                dve.wait_ge(s_chain, links[0])

            def chunk_max(n):
                c, slot = chunks[n][0], chunks[n][2]
                dve.wait_ge(s_wload[slot], w_arrival[n][1])
                dve.tensor_reduce(w_max[:, c:c + 1], stage(n), AX_X, ALU.max, apply_absolute_value=True)\
                   .then_inc(s_wmax, 1)

            def chunk_scale(n):
                c = slice(chunks[n][0], chunks[n][0] + 1)
                dve.wait_ge(s_wtop, n + 1)
                link(dve.tensor_scalar(w_top[:, c], w_top[:, c], 2.0 ** -100, None, ALU.max))
                link(dve.tensor_scalar(w_exp[:, c].bitcast(U32), w_top[:, c].bitcast(U32), EXPONENT, None,
                                       ALU.bitwise_and))
                link(dve.reciprocal(w_inv[:, c], w_exp[:, c]))
                dve.tensor_scalar(w_scale[:, c], w_inv[:, c], W_SCALE, None, ALU.mult).then_inc(s_wscale, 1)

            def chunk_lo(n):
                c, _, _, _, hi, lo = chunks[n]
                dve.wait_ge(s_whi, n + 1)
                dve.scalar_tensor_tensor(out=lo.rearrange("p c o -> p (c o)"), in0=stage(n),
                                         scalar=w_scale[:, c:c + 1], in1=hi.rearrange("p c o -> p (c o)"),
                                         op0=ALU.mult, op1=ALU.subtract).then_inc(s_wready, 1)

            def row_stats(row_tile, n, r):
                for h in range(2):
                    ins = dve.bn_stats(stats[:, h, :], row_tile[:, HALF * h:HALF * h + HALF])
                ins.then_inc(s_stat, 1)
                dve.wait_ge(s_stat, 2 * n + 1)
                alone(dve)
                dve.bn_aggr(moments[:, r], stats[:, :, :].rearrange("p a b -> p (a b)")).then_inc(s_stat, 1)
                dve.wait_ge(s_stat, 2 * n + 2)
                dve.tensor_scalar(var_scaled[:, r:r + 1], moments[:, r, 1:2], EPS,
                                  XN_SCALE ** -2, ALU.add, ALU.mult).then_inc(s_var, 1)

            def normalise(row_tile, n, r):
                dve.wait_ge(s_rstd, n + 1)
                dve.tensor_scalar(row_tile, row_tile, moments[:, r, 0:1], rstd[:, r:r + 1],
                                  ALU.subtract, ALU.mult).then_inc(s_norm, 1)

            def turned_lo(t):
                for q in range(4):
                    u, h = q // 2, q % 2
                    dve.wait_ge(s_xthi, 4 * t + q + 1)
                    dst = (slice(None), slice(4 * h, 4 * h + 4), slice(P * u, P * u + P))
                    dve.tensor_tensor(xn[:, 1][dst], B_XT[q][:, :].rearrange("p (c n) -> p c n", c=4),
                                      xn[:, 0][dst], ALU.subtract).then_inc(s_xn, 1)

            def low(dst, src, factor, hi, n_hi):
                dve.wait_ge(s_dhi, n_hi)
                dve.scalar_tensor_tensor(out=dst, in0=src, scalar=factor, in1=hi, op0=ALU.mult, op1=ALU.subtract)\
                   .then_inc(s_dread, 1)

            def q_lo(t, m):
                low(q_part[:, (m // 2) % 2, 1, m % 2], B_DENSE[m % 2][:, 0:AB], Q_FACTOR,
                    q_part[:, (m // 2) % 2, 0, m % 2], 12 * t + m + 1)

            def k_lo(t, b):
                low(k_part[:, 1, b], B_DENSE[b][:, 0:AB], KV_FACTOR, k_part[:, 0, b], 12 * t + GROUPS + b + 1)

            def v_lo(t, u):
                low(v_aug[:, 1, u, :, 0:DH], B_DENSE[u][:, 0:KV].rearrange("p (g w) -> p g w", g=GROUPS), KV_FACTOR,
                    v_aug[:, 0, u, :, 0:DH], 12 * t + GROUPS + 2 + u + 1)

            def row_maxima(a, m):
                for u in range(U):
                    if u == 0 and m >= 4:
                        dve.wait_ge(s_pt, 16 * a + 2 * m - 6)
                    dve.wait_ge(s_score, 16 * a + 2 * m + u + 1)
                    alone(dve)
                    for j in range(HPG):
                        ins = dve.tensor_tensor_reduce(
                            score[:, m % 4, u, SEQ * j:SEQ * j + SEQ], B_SCORE[u][:, SEQ * j:SEQ * j + SEQ],
                            mask_add[:, :], 1.0, MASKED * 2, ALU.add, ALU.max,
                            row_max[:, m % 4, HPG * u + j:HPG * u + j + 1])
                    ins.then_inc(s_sread, 1)
                dve.wait_ge(s_sread, 16 * a + 2 * m + 2)
                dve.tensor_scalar(neg_max[:, m % 4, :], row_max[:, m % 4, :], c_neg[:, m:m + 1], None, ALU.mult)\
                   .then_inc(s_neg, 1)

            def prob_lo(a, m):
                for u in range(U):
                    dve.wait_ge(s_pthi, 16 * a + 2 * m + u + 1)
                    dve.tensor_tensor(prob_t[:, m % 2, 1, u], B_TURN[u][:, :], prob_t[:, m % 2, 0, u], ALU.subtract)\
                       .then_inc(s_ptread, 1)

            def divide(a, m):
                av = B_AV[:, 0:VW * U * HPG].rearrange("p (h w) -> p h w", w=VW)
                dve.wait_ge(s_av, 8 * a + m + 1)
                dve.reciprocal(inv_sum[:, :].rearrange("p (h o) -> p h o", o=1), av[:, :, DH:DH + 1]).then_inc(s_inv, 1)
                dve.wait_ge(s_inv, 8 * a + m + 1)
                if m >= 2:
                    dve.wait_ge(s_ot, 8 * a + m - 1)
                dve.tensor_tensor(attn[:, m % 2, :].rearrange("p (h w) -> p h w", w=DH), av[:, :, 0:DH],
                                  inv_sum[:, :].rearrange("p (h o) -> p h o", o=1).broadcast_to([P, U * HPG, DH]),
                                  ALU.mult).then_inc(s_avread, 1)

            def attn_lo(a, m):
                dve.wait_ge(s_othi, 8 * a + m + 1)
                dve.tensor_tensor(attn_t[:, 1, m], B_ATTN_T[:, 0:AB], attn_t[:, 0, m], ALU.subtract).then_inc(s_otread, 1)

            def residual(t, k0):
                for q in range(4):
                    u, h = q // 2, q % 2
                    if q == 0:
                        dve.wait_ge(s_xres, 16 * t)
                    dve.wait_ge(s_dense, dense0(t) + k0 + q + 1)
                    cols = x_res[:, u, HALF * h:HALF * h + HALF]
                    dve.scalar_tensor_tensor(out=cols, in0=B_DENSE[q % 2][:, :], scalar=c_out[:, h:h + 1], in1=cols,
                                             op0=ALU.mult, op1=ALU.add).then_inc(s_dread, 1)

            def block_scales(t):
                dve.wait_ge(s_dread, dense0(t))
                dve.tensor_scalar(c_score[:, :], score_base[:, :], ctx_exp[:, 0:1], None, ALU.mult)
                dve.tensor_scalar(c_neg[:, :], score_base[:, :], ctx_exp[:, 0:1], -1.0, ALU.mult, ALU.mult)
                dve.tensor_scalar(c_out[:, :], out_base[:, :], ctx_exp[:, 0:1], None, ALU.mult).then_inc(s_scales, 1)
                dve.wait_ge(s_scales, t)

            def ctx_max_of(t):
                dve.wait_ge(s_ctxload, 16 * t + 16)
                dve.tensor_reduce(ctx_max[:, :], ctx_in[:, :], AX_X, ALU.max, apply_absolute_value=True)\
                   .then_inc(s_ctxmax, 1)

            def ctx_scale_of(t):
                dve.wait_ge(s_ctxtop, t + 1)
                dve.tensor_scalar(ctx_top[:, :], ctx_top[:, :], 2.0 ** -100, None, ALU.max).then_inc(s_ctxstep, 1)
                dve.wait_ge(s_ctxstep, 3 * t + 1)
                dve.tensor_scalar(ctx_exp[:, :].bitcast(U32), ctx_top[:, :].bitcast(U32), EXPONENT, None,
                                  ALU.bitwise_and).then_inc(s_ctxstep, 1)
                dve.wait_ge(s_ctxstep, 3 * t + 2)
                dve.reciprocal(ctx_inv[:, :], ctx_exp[:, :]).then_inc(s_ctxstep, 1)
                dve.wait_ge(s_ctxstep, 3 * t + 3)
                dve.tensor_scalar(ctx_scale[:, :], ctx_inv[:, :], W_SCALE, None, ALU.mult).then_inc(s_ctxscale, 1)

            def iteration(t, project, attend, chunk_at_step=None):
                a = t - 1
                if attend:
                    block_scales(t)
                for s in range(STEPS):
                    if chunk_at_step is not None and 1 <= s <= GROUPS:
                        chunk_max(chunk_at_step + s - 1)
                        chunk_scale(chunk_at_step + s - 1)
                    if attend and s < GROUPS:
                        row_maxima(a, s)
                    if project and s == 1:
                        ctx_max_of(t)
                    if project and s == 2:
                        ctx_scale_of(t)
                    if attend and 2 <= s < GROUPS + 2:
                        prob_lo(a, s - 2)
                    if attend and 3 <= s < GROUPS + 3:
                        divide(a, s - 3)
                    if attend and 4 <= s:
                        attn_lo(a, s - 4)
                    if project and 1 <= s <= GROUPS:
                        q_lo(t, s - 1)
                    if project and s in (GROUPS, GROUPS + 1):
                        if s == GROUPS:
                            dve.wait_ge(s_xload, 16 * t + 32)
                        row_stats(x_in[:, s - GROUPS], 2 * t + 2 + s - GROUPS, s - GROUPS)
                    if project and s in (GROUPS + 1, GROUPS + 2):
                        normalise(x_in[:, s - GROUPS - 1], 2 * t + 1 + s - GROUPS, s - GROUPS - 1)
                    if project and s in (GROUPS + 1, GROUPS + 2):
                        k_lo(t, s - GROUPS - 1)
                    if chunk_at_step is not None and 1 <= s <= GROUPS:
                        chunk_lo(chunk_at_step + s - 1)
                if project:
                    v_lo(t, 0)
                    v_lo(t, 1)
                    turned_lo(t + 1)
                if attend:
                    residual(t, 12 if project else 0)

            dve.wait_ge(s_xload, 16)
            for u in range(U):
                row_stats(x_in[:, u], u, u)
            for u in range(U):
                normalise(x_in[:, u], u, u)
            dve.wait_ge(s_mask, 16)
            link(dve.tensor_scalar(mask_add[:, :], mask_u8[:, :], -1.0, -MASKED, ALU.add, ALU.mult))
            chunk_max(0)
            chunk_scale(0)
            turned_lo(0)
            chunk_max(1)
            chunk_scale(1)
            chunk_lo(0)
            for m in range(GROUPS):
                chunk_max(m + 2)
                chunk_scale(m + 2)
                chunk_lo(m + 1)
                q_lo(0, m)
            chunk_lo(CH_O - 1)
            ctx_max_of(0)
            ctx_scale_of(0)
            link(dve.tensor_scalar(score_base[:, :], w_exp[:, CH_Q:CH_Q + GROUPS], w_exp[:, CH_K:CH_K + 1], C_SCORE,
                                   ALU.mult, ALU.mult))
            dve.wait_ge(s_xload, 32)
            for u in range(U):
                row_stats(x_in[:, u], 2 + u, u)
            for u in range(U):
                normalise(x_in[:, u], 2 + u, u)
            for b in range(2):
                k_lo(0, b)
            for u in range(U):
                v_lo(0, u)
            turned_lo(1)
            for n in range(CH_O, CH_12):
                chunk_max(n)
                chunk_scale(n)
                chunk_lo(n)
            link(dve.tensor_scalar(out_base[:, :], w_exp[:, CH_O:CH_O + 2], w_exp[:, CH_V:CH_V + 1], C_OUT,
                                   ALU.mult, ALU.mult))
            with dve.Fori(1, NB) as t:
                iteration(t, True, True)
            iteration(NB, False, True, chunk_at_step=CH_12)

            dve.wait_ge(s_b12, 16)
            e12 = w_exp[:, CH_12:CH_12 + MC]
            dve.tensor_reduce(bound[:, 1:2], b12[:, :], AX_X, ALU.max, apply_absolute_value=True).then_inc(s_bmax, 1)
            dve.tensor_scalar(c_hid[:, :], e12, C_HID, None, ALU.mult).then_inc(s_yread, 8)
            dve.wait_ge(s_yread, 8)
            link(dve.reciprocal(c_hid_inv[:, :], c_hid[:, :]))
            link(dve.tensor_tensor(b2_scaled[:, :], b12[:, MC:2 * MC], c_hid_inv[:, :], ALU.mult))
            link(dve.tensor_reduce(bound[:, 0:1], e12, AX_X, ALU.max))
            link(dve.tensor_scalar(bound[:, 7:8], bound[:, 0:1], 2.0 ** 11, None, ALU.mult))
            dve.wait_ge(s_btop, 1)
            link(dve.tensor_tensor(bound[:, 3:4], bound[:, 7:8], bound[:, 2:3], ALU.add))
            link(dve.tensor_tensor(bound[:, 4:5], bound[:, 3:4], bound[:, 3:4], ALU.mult))
            link(dve.tensor_scalar(bound[:, 5:6].bitcast(U32), bound[:, 4:5].bitcast(U32), EXPONENT, None,
                                   ALU.bitwise_and))
            link(dve.reciprocal(bound[:, 6:7], bound[:, 5:6]))
            dve.tensor_scalar(hid_scale[:, :], c_hid[:, :], bound[:, 6:7], W_SCALE, ALU.mult, ALU.mult)\
               .then_inc(s_const, 1)

            def y_stats(f, u):
                if u == 0:
                    dve.wait_ge(s_yload, 16 * f + 16)
                row_stats(y_in[:, u], 2 * (NB + 1) + FT * f + u, u % 2)

            def y_norm(f, u):
                normalise(y_in[:, u], 2 * (NB + 1) + FT * f + u, u % 2)

            def y_lo(f):
                for q in range(8):
                    dve.wait_ge(s_ythi, 8 * f + q + 1)
                    dst = (slice(None), slice(4 * (q % 2), 4 * (q % 2) + 4), slice(P * (q // 2), P * (q // 2) + P))
                    dve.tensor_tensor(yn[:, 1][dst], B_XT[q % 4][:, :].rearrange("p (c n) -> p c n", c=4),
                                      yn[:, 0][dst], ALU.subtract).then_inc(s_yn, 1)

            for u in range(FT):
                y_stats(0, u)
                if u:
                    y_norm(0, u - 1)
            y_norm(0, FT - 1)
            y_lo(0)
            for n in range(CH_3, NW):
                chunk_max(n)
                chunk_scale(n)
                chunk_lo(n)
            dve.tensor_scalar(c_ffn[:, :], w_exp[:, CH_3:CH_3 + 2], bound[:, 5:6], C_FFN, ALU.mult, ALU.mult)\
               .then_inc(s_const3, 1)
            dve.wait_ge(s_const3, 1)
            with dve.Fori(0, NF) as f:
                for m in range(MC):
                    dve.wait_ge(s_h, 16 * f + 2 * m + 2)
                    dve.wait_ge(s_silu, 8 * f + m + 1)
                    dve.scalar_tensor_tensor(out=gated[:, m % 2], in0=B_FFN[2 * (m % 2) + 1][:, :],
                                             scalar=b2_scaled[:, m:m + 1], in1=silu[:, m % 2], op0=ALU.add,
                                             op1=ALU.mult).then_inc(s_gated, 1)
                    dve.wait_ge(s_hhi, 8 * f + m + 1)
                    dve.scalar_tensor_tensor(out=hid[:, 1, m], in0=gated[:, m % 2], scalar=hid_scale[:, m:m + 1],
                                             in1=hid[:, 0, m], op0=ALU.mult, op1=ALU.subtract).then_inc(s_hid, 1)
                    if 2 <= m < 2 + FT:
                        y_stats(f + 1, m - 2)
                    if 3 <= m < 3 + FT:
                        y_norm(f + 1, m - 3)
                y_lo(f + 1)
                dve.wait_ge(s_yresb, f + 1)
                for q in range(8):
                    u, h = q // 2, q % 2
                    dve.wait_ge(s_y, 8 * f + q + 1)
                    cols = y_res[:, u, HALF * h:HALF * h + HALF]
                    dve.scalar_tensor_tensor(out=cols, in0=B_FFN[q % 4][:, :], scalar=c_ffn[:, h:h + 1], in1=cols,
                                             op0=ALU.mult, op1=ALU.add).then_inc(s_yread, 1)


_OUT = (16, 128, 1024)


def kernel(x, ctx_4096, mask_SxS2_bk0, L0_xattn_w_q, L0_xattn_w_k, L0_xattn_w_v, L0_xattn_w_out, L0_ffn_w12,
           L0_ffn_b12, L0_ffn_w3, L0_ffn_b3):
    import numpy as np
    import concourse.bacc as bacc
    from concourse.bass_utils import run_bass_kernel_spmd

    def cols(w, n):
        w = np.asarray(w)
        return np.ascontiguousarray(w.reshape(w.shape[0] // n, n, KC, P).transpose(0, 3, 2, 1))\
            .reshape(w.shape[0] // n, P, KC * n)

    w12 = np.asarray(L0_ffn_w12).reshape(2, MC, P, D).transpose(1, 0, 2, 3).reshape(2 * M, D)
    ctx = np.asarray(ctx_4096).reshape(NB, AB, KC, P).transpose(0, 3, 2, 1)
    arrays = {
        "x": np.ascontiguousarray(np.asarray(x).reshape(TOK, D)),
        "ctx_t": np.ascontiguousarray(ctx).reshape(NB, P, KC * AB),
        "mask": np.ascontiguousarray(mask_SxS2_bk0),
        "wq_t": cols(L0_xattn_w_q, P),
        "wk_t": cols(L0_xattn_w_k, KV)[0],
        "wv_t": cols(L0_xattn_w_v, KV)[0],
        "wo_t": cols(L0_xattn_w_out, HALF),
        "w12_t": cols(w12, 2 * P),
        "b12_t": np.ascontiguousarray(np.asarray(L0_ffn_b12).reshape(2 * MC, P).T),
        "w3_t": cols(L0_ffn_w3, HALF),
        "b3_row": np.ascontiguousarray(np.asarray(L0_ffn_b3).reshape(1, D)),
    }
    nc = bacc.Bacc("TRN2", target_bir_lowering=False, num_devices=1)
    args = [nc.dram_tensor(name, a.shape, mybir.dt.from_np(a.dtype), kind="ExternalInput").ap()
            for name, a in arrays.items()]
    out = nc.dram_tensor("out", (TOK, D), F32, kind="ExternalOutput").ap()
    xattn_ffn(nc, *args, out)
    r = run_bass_kernel_spmd(nc, [arrays], core_ids=[0])
    return r.results[0]["out"].reshape(_OUT)
```

```python
from contextlib import ExitStack

import concourse.bass as bass
from concourse import mybir

F32 = mybir.dt.float32
F16 = mybir.dt.float16
U32 = mybir.dt.uint32
U8 = mybir.dt.uint8
ALU = mybir.AluOpType
ACT = mybir.ActivationFunctionType
AX_X = mybir.AxisListType.X
RMAX = bass.bass_isa.ReduceOp.max

P = 128
D = 1024
KC = D // P
SEQ = 128
HEADS, GROUPS, DH = 32, 8, 32
HPG = HEADS // GROUPS
KV = GROUPS * DH
TOK = 16 * SEQ
U = 2
AB = U * SEQ
NB = TOK // AB
FB = 512
NF = TOK // FB
FT = FB // P
M = D
MC = M // P
HALF = 512
EPS = 1e-5
VW = DH + 2
EXPONENT = 0x7F800000
MASKED = -(2.0 ** 100)
XN_SCALE = 2.0 ** 8
W_SCALE = 2.0 ** 13
Q_FACTOR = 2.0 ** -15 * DH ** -0.5
KV_FACTOR = 2.0 ** -23
C_SCORE = 2.0 ** -9
C_OUT = 2.0 ** -16
C_HID = 2.0 ** -21
C_FFN = 2.0 ** -26
NDMA_STACK = 12


def xattn_ffn(nc, x, ctx_t, mask, wq_t, wk_t, wv_t, wo_t, w12_t, b12_t, w3_t, b3_row, out):
    x_blocks = x.rearrange("(b u p) d -> b p u d", b=NB, p=P)
    x1_dram = nc.dram_tensor("x1_scratch", (TOK, D), F32, kind="Internal").ap()
    x1_blocks = x1_dram.rearrange("(b u p) d -> b p u d", b=NB, p=P)
    x1_ffn = x1_dram.rearrange("(b u p) d -> b p u d", b=NF, p=P)
    out_ffn = out.rearrange("(b u p) d -> b p u d", b=NF, p=P)

    def at(blocks, i):
        return blocks[bass.ds(i, 1)].rearrange("o p u d -> (o p) u d")

    with ExitStack() as stack:
        def sb(name, shape, dt):
            return stack.enter_context(nc.sbuf_tensor(name, shape, dt))

        def sem(name):
            return stack.enter_context(nc.semaphore(name))

        arena_in = sb("arena_in", [P, 32768], F16)
        arena_out = sb("arena_out", [P, 16384], F16)
        arena_work = sb("arena_work", [P, 32768], F16)
        wstage = sb("wstage", [P, 4096], F32)

        def carve(arena, at_, n, dt=F16):
            w = n * (2 if dt is F32 else 1)
            v = arena[:, at_:at_ + w]
            return (v.bitcast(dt) if dt is F32 else v), at_ + w

        o = 0
        wq, o = carve(arena_in, o, 2 * GROUPS * KC * P)
        wq = wq.rearrange("p (s m c o) -> p s m c o", s=2, m=GROUPS, c=KC)
        ctx_in, o = carve(arena_in, o, KC * AB, F32)
        wk, o = carve(arena_in, o, 2 * KC * KV)
        wk = wk.rearrange("p (s c o) -> p s c o", s=2, c=KC)
        wv, o = carve(arena_in, o, 2 * KC * KV)
        wv = wv.rearrange("p (s c o) -> p s c o", s=2, c=KC)
        ctx, o = carve(arena_in, o, 2 * KC * AB)
        ctx = ctx.rearrange("p (s c n) -> p s c n", s=2, c=KC)
        wo = arena_out[:, :].rearrange("p (h s c o) -> p h s c o", h=2, s=2, c=KC)
        w12 = arena_in[:, :].rearrange("p (m s c o) -> p m s c o", m=MC, s=2, c=KC)
        w3 = wo

        o = 0
        x_in, o = carve(arena_work, o, U * D, F32)
        x_in = x_in.rearrange("p (u d) -> p u d", u=U)
        x_res, o = carve(arena_work, o, U * D, F32)
        x_res = x_res.rearrange("p (u d) -> p u d", u=U)
        xn, o = carve(arena_work, o, 2 * KC * AB)
        xn = xn.rearrange("p (s c n) -> p s c n", s=2, c=KC)
        q_part, o = carve(arena_work, o, 2 * 2 * 2 * AB)
        q_part = q_part.rearrange("p (r s g n) -> p r s g n", r=2, s=2, g=2)
        k_part, o = carve(arena_work, o, 2 * 2 * AB)
        k_part = k_part.rearrange("p (s b n) -> p s b n", s=2, b=2)
        o = 2 * FT * D + 2 * KC * FB
        q_stack, o = carve(arena_work, o, HEADS * AB)
        q_stack = q_stack.rearrange("p (g j n) -> p g j n", g=GROUPS, j=HPG)
        k_stack, o = carve(arena_work, o, GROUPS * AB)
        k_stack = k_stack.rearrange("p (b g n) -> p b g n", b=2, g=GROUPS // 2)
        v_aug, o = carve(arena_work, o, 2 * U * GROUPS * VW)
        v_aug = v_aug.rearrange("p (s u g w) -> p s u g w", s=2, u=U, g=GROUPS)
        attn_t, o = carve(arena_work, o, 2 * GROUPS * AB)
        attn_t = attn_t.rearrange("p (s g n) -> p s g n", s=2, g=GROUPS)
        assert o <= arena_work.shape[1], o
        score = sb("score", [P, 4, U, HPG * SEQ], F32)
        prob_t = sb("prob_t", [P, 2, 2, U, HPG * SEQ], F16)
        attn = sb("attn", [P, 2, U * HPG * DH], F32)

        o = 0
        y_in, o = carve(arena_work, o, FT * D, F32)
        y_in = y_in.rearrange("p (u d) -> p u d", u=FT)
        yn, o = carve(arena_work, o, 2 * KC * FB)
        yn = yn.rearrange("p (s c n) -> p s c n", s=2, c=KC)
        hid, o = carve(arena_work, o, 2 * MC * FB)
        hid = hid.rearrange("p (s c n) -> p s c n", s=2, c=MC)
        y_res, o = carve(arena_work, o, FT * D, F32)
        y_res = y_res.rearrange("p (u d) -> p u d", u=FT)
        assert o <= arena_work.shape[1], o
        silu = prob_t[:, :, :, :, :].rearrange("p a b c d -> p (a b c d)")[:, 0:2 * 2 * FB].bitcast(F32) \
            .rearrange("p (r n) -> p r n", r=2)
        gated = score[:, 0, :, :]
        b3_all = score[:, 2, :, :].rearrange("p u n -> p (u n)")

        ident = sb("ident", [P, P], F32)
        mask_u8 = sb("mask_u8", [P, SEQ], U8)
        mask_add = sb("mask_add", [P, SEQ], F32)
        b12 = sb("b12", [P, 2 * MC], F32)
        b2_scaled = sb("b2_scaled", [P, MC], F32)
        NW = GROUPS + 2 + 4 + MC + 4
        CH_Q, CH_K, CH_V, CH_O = 0, GROUPS, GROUPS + 1, GROUPS + 2
        CH_12, CH_3 = CH_O + 4, CH_O + 4 + MC
        w_max = sb("w_max", [P, NW], F32)
        w_top = sb("w_top", [P, NW], F32)
        w_exp = sb("w_exp", [P, NW], F32)
        w_inv = sb("w_inv", [P, NW], F32)
        w_scale = sb("w_scale", [P, NW], F32)
        ctx_max = sb("ctx_max", [P, 1], F32)
        ctx_top = sb("ctx_top", [P, 1], F32)
        ctx_exp = sb("ctx_exp", [P, 1], F32)
        ctx_inv = sb("ctx_inv", [P, 1], F32)
        ctx_scale = sb("ctx_scale", [P, 1], F32)
        score_base = sb("score_base", [P, GROUPS], F32)
        out_base = sb("out_base", [P, 4], F32)
        c_score = sb("c_score", [P, GROUPS], F32)
        c_neg = sb("c_neg", [P, GROUPS], F32)
        c_out = sb("c_out", [P, 4], F32)
        ctx_exp_kept = sb("ctx_exp_kept", [P, 1], F32)
        c_hid = sb("c_hid", [P, MC], F32)
        c_hid_inv = sb("c_hid_inv", [P, MC], F32)
        hid_scale = sb("hid_scale", [P, MC], F32)
        c_ffn = sb("c_ffn", [P, 4], F32)
        bound = sb("bound", [P, 8], F32)
        row_max = sb("row_max", [P, 4, U * HPG], F32)
        neg_max = sb("neg_max", [P, 4, U * HPG], F32)
        inv_sum = sb("inv_sum", [P, U * HPG], F32)
        stats = sb("stats", [P, 2, 6], F32)
        moments = sb("moments", [P, 2, 2], F32)
        var_scaled = sb("var_scaled", [P, 2], F32)
        rstd = sb("rstd", [P, 2], F32)
        minus_half = sb("minus_half", [P, 1], F32)

        bank = [stack.enter_context(nc.psum_tensor(f"bank{i}", [P, HALF], F32)) for i in range(8)]
        B_SCORE, B_TURN, B_AV, B_ATTN_T, B_DENSE = bank[0:2], bank[2:4], bank[4], bank[5], bank[6:8]
        B_FFN = bank[4:8]
        B_XT = bank[0:4]

        s_mask, s_b12, s_b3 = sem("mask_loaded"), sem("b12_loaded"), sem("b3_loaded")
        s_wload = [sem(f"weights_loaded_{i}") for i in range(8)]
        s_wmax, s_wtop, s_wscale = sem("w_max_done"), sem("w_top_done"), sem("w_scale_done")
        s_whi, s_wready = sem("w_hi_done"), sem("w_ready")
        s_ident, s_vinit, s_maskadd = sem("ident_done"), sem("v_init_done"), sem("mask_add_done")
        s_xload, s_ctxload, s_xres = sem("x_loaded"), sem("ctx_loaded"), sem("x_res_loaded")
        s_ctxmax, s_ctxtop, s_ctxscale, s_ctx = sem("ctx_max_done"), sem("ctx_top_done"), sem("ctx_scale_done"), sem("ctx_ready")
        s_ctxhi = sem("ctx_hi_done")
        s_norm, s_stat, s_var, s_rstd = sem("norm_done"), sem("stats_done"), sem("var_done"), sem("rstd_done")
        s_xt, s_xthi, s_xn = sem("x_turned"), sem("xn_hi_done"), sem("xn_ready")
        s_dense, s_dhi, s_dread = sem("dense_done"), sem("dense_hi_done"), sem("dense_read")
        s_qst = [sem("q_stack_loaded_0"), sem("q_stack_loaded_1")]
        s_kst = sem("k_stack_loaded")
        s_score, s_sread, s_neg, s_prob = sem("score_done"), sem("score_read"), sem("neg_max_done"), sem("prob_done")
        s_pt, s_pthi, s_ptread = sem("prob_turned"), sem("prob_t_hi_done"), sem("prob_t_ready")
        s_av, s_inv, s_avread = sem("av_done"), sem("inv_sum_done"), sem("attn_ready")
        s_ot, s_othi, s_otread = sem("attn_turned"), sem("attn_t_hi_done"), sem("attn_t_ready")
        s_cout, s_x1 = sem("c_out_done"), sem("x1_stored")
        s_chain, s_alone = sem("vector_chain"), sem("waits_alone")
        s_const, s_const3 = sem("ffn_consts_done"), sem("ffn_out_consts_done")
        s_scales, s_ctxstep = sem("block_scales_done"), sem("ctx_step_done")
        s_bmax, s_btop = sem("b_max_done"), sem("b_top_done")
        s_yload, s_yres, s_yresb = sem("y_loaded"), sem("y_res_loaded"), sem("y_res_with_b3")
        s_yt, s_ythi, s_yn = sem("y_turned"), sem("yn_hi_done"), sem("yn_ready")
        s_h, s_silu, s_gated, s_hhi, s_hid = sem("h_done"), sem("silu_done"), sem("gated_done"), sem("hid_hi_done"), sem("hid_ready")
        s_y, s_yread, s_out = sem("y_done"), sem("ffn_bank_read"), sem("out_stored")

        block = stack.enter_context(nc.Block())

        def dense0(t):
            return 0 if isinstance(t, int) and t == 0 else 16 * t - 4

        STEPS = GROUPS + 4

        def alone(engine):
            engine.sem_inc(s_alone, 1)

        chunks = []
        for m in range(GROUPS):
            chunks.append((CH_Q + m, wq_t[m], m, 1, wq[:, 0, m], wq[:, 1, m]))
        chunks.append((CH_K, wk_t, 0, 2, wk[:, 0], wk[:, 1]))
        chunks.append((CH_V, wv_t, 2, 2, wv[:, 0], wv[:, 1]))
        for k in range(4):
            quarter = [wo[:, k // 2, part, :, 256 * (k % 2):256 * (k % 2) + 256] for part in range(2)]
            chunks.append((CH_O + k, wo_t[k], 2 * (k % 2), 2, quarter[0], quarter[1]))
        for m in range(MC):
            chunks.append((CH_12 + m, w12_t[m], 2 * (m % 2), 2, w12[:, m, 0], w12[:, m, 1]))
        for k in range(4):
            quarter = [w3[:, k // 2, part, :, 256 * (k % 2):256 * (k % 2) + 256] for part in range(2)]
            chunks.append((CH_3 + k, w3_t[k], 2 * (k % 2), 2, quarter[0], quarter[1]))
        last_user, w_arrival, loads = [None] * 8, [], [0] * 8
        for n, (_, _, slot, width, _, _) in enumerate(chunks):
            free_after = [last_user[s] for s in range(slot, slot + width) if last_user[s] is not None]
            for s in range(slot, slot + width):
                last_user[s] = n
            loads[slot] += 16
            w_arrival.append((max(free_after) + 1 if free_after else 0, loads[slot]))

        def stage(n):
            _, _, slot, width, _, _ = chunks[n]
            if slot >= 4:
                return score[:, slot - 4, :, :].rearrange("p u n -> p (u n)")
            return wstage[:, slot * 1024:(slot + width) * 1024]

        W_OUT_AT = (CH_O, 4, {GROUPS - 1: 0, GROUPS + 1: 1, GROUPS + 3: 2}, (3, 4))
        W12_AT = (CH_12, MC, {GROUPS - 1: 0, GROUPS + 1: 1, GROUPS + 3: 2}, ())
        W12_AT_END = (CH_12, MC, {0: 3, 1: 4, 2: 5, 3: 6}, (7, 8))
        NO_SPLIT = (None, 0, {}, ())

        def rows_dst(t):
            if isinstance(t, int) and t >= NB:
                return yn[:, :, :, AB * (t - NB):AB * (t - NB) + AB]
            return xn

        @block.sync
        def _(sp):
            def load_chunk(n):
                if w_arrival[n][0]:
                    sp.wait_ge(s_wready, w_arrival[n][0])
                sp.dma_start(stage(n), chunks[n][1]).then_inc(s_wload[chunks[n][2]], 16)

            def load_ctx(t):
                sp.wait_ge(s_ctx, 4 * t)
                alone(sp)
                sp.dma_start(ctx_in[:, :], ctx_t[bass.ds(t, 1)].rearrange("o p n -> (o p) n")).then_inc(s_ctxload, 16)

            def stack_q(t, pair):
                sp.wait_ge(s_dread, dense0(t) + 2 * pair + 2)
                for j in range(HPG):
                    for r, part in ((0, 0), (1, 1), (2, 0)):
                        sp.dma_start(q_stack[DH * r:DH * r + DH, 2 * pair:2 * pair + 2, j, :],
                                     q_part[DH * j:DH * j + DH, pair % 2, part]).then_inc(s_qst[pair % 2], 16)

            def stack_k(t):
                sp.wait_ge(s_dread, dense0(t) + GROUPS + 2)
                for g in range(4):
                    for r, part in ((0, 0), (1, 0), (2, 1)):
                        sp.dma_start(k_stack[DH * r:DH * r + DH, :, g, :],
                                     k_part[DH * g:DH * g + DH, part]).then_inc(s_kst, 16)

            def load_x(t):
                sp.wait_ge(s_xt, 4 * t)
                alone(sp)
                rows = at(x1_blocks, t - NB) if isinstance(t, int) and t >= NB else at(x_blocks, t)
                sp.dma_start(x_in, rows).then_inc(s_xload, 16)

            def store_x1(t):
                sp.wait_ge(s_dread, dense0(t + 1) if not (isinstance(t, int) and t == NB) else dense0(t) + 4)
                alone(sp)
                sp.dma_start(at(x1_blocks, t - 1), x_res).then_inc(s_x1, 16)
                if not (isinstance(t, int) and t == NB):
                    sp.wait_ge(s_x1, 16 * t)
                    alone(sp)
                    sp.dma_start(x_res, at(x_blocks, t)).then_inc(s_xres, 16)

            def iteration(t, early=(), late=(), tail=()):
                load_x(t + 1)
                for n in early:
                    load_chunk(n)
                for pair in range(GROUPS // 2):
                    sp.wait_ge(s_score, 16 * (t - 1) + 4 * pair + 4)
                    alone(sp)
                    stack_q(t, pair)
                    if pair == 2 and not (isinstance(t, int) and t == NB - 1):
                        load_ctx(t + 1)
                for n in late:
                    load_chunk(n)
                sp.wait_ge(s_score, 16 * t)
                alone(sp)
                stack_k(t)
                for n in tail:
                    load_chunk(n)

            sp.dma_start(x_in, at(x_blocks, 0)).then_inc(s_xload, 16)
            load_chunk(0)
            load_chunk(1)
            sp.dma_start(mask_u8[:, :], mask).then_inc(s_mask, 16)
            load_chunk(2)
            load_chunk(3)
            sp.dma_start(ctx_in[:, :], ctx_t[0]).then_inc(s_ctxload, 16)
            for n in range(4, GROUPS):
                load_chunk(n)
            load_x(1)
            load_chunk(CH_K)
            stack_q(0, 0)
            load_chunk(CH_V)
            for pair in range(1, GROUPS // 2):
                stack_q(0, pair)
            stack_k(0)
            load_ctx(1)
            sp.dma_start(x_res, at(x_blocks, 0)).then_inc(s_xres, 16)
            sp.dma_start(b12[:, :], b12_t).then_inc(s_b12, 16)
            load_chunk(CH_O)
            load_chunk(CH_O + 1)
            iteration(1, late=(CH_O + 2,), tail=(CH_O + 3,))
            store_x1(1)
            with sp.Fori(2, NB - 1) as t:
                iteration(t)
                store_x1(t)
            iteration(NB - 1, early=(CH_12, CH_12 + 1), late=(CH_12 + 2,), tail=(CH_12 + 3,))
            load_x(NB + 1)
            for n in range(CH_12 + 4, CH_3):
                load_chunk(n)
            store_x1(NB - 1)
            store_x1(NB)

            def ffn_block(f, prefetch):
                if prefetch:
                    if isinstance(f, int) and f == 0:
                        sp.wait_ge(s_xt, 4 * (NB + 2))
                        sp.wait_ge(s_x1, 16 * NB)
                    else:
                        sp.wait_ge(s_yt, 8 * f)
                        alone(sp)
                    sp.dma_start(y_in, at(x1_ffn, f + 1)).then_inc(s_yload, 16)
                if isinstance(f, int) and f == 0:
                    for n in range(CH_3 + 2, NW):
                        load_chunk(n)
                for u in range(FT):
                    sp.wait_ge(s_yread, 8 * f + 2 * u + 2)
                    alone(sp)
                    sp.dma_start(at(out_ffn, f)[:, u], y_res[:, u]).then_inc(s_out, 16)
                sp.wait_ge(s_out, 16 * FT * (f + 1))
                alone(sp)
                if prefetch:
                    sp.dma_start(y_res, at(x1_ffn, f + 1)).then_inc(s_yres, 16)

            load_chunk(CH_3)
            load_chunk(CH_3 + 1)
            sp.wait_ge(s_pt, 16 * NB)
            sp.dma_start(b3_all, b3_row.broadcast_to([P, D])).then_inc(s_b3, 16)
            sp.wait_ge(s_dense, dense0(NB) + 4)
            sp.dma_start(y_res, at(x1_ffn, 0)).then_inc(s_yres, 16)
            ffn_block(0, True)
            with sp.Fori(1, NF - 1) as f:
                ffn_block(f, True)
            ffn_block(NF - 1, False)

        @block.gpsimd
        def _(pool):
            def top(n):
                pool.wait_ge(s_wmax, n + 1)
                pool.partition_all_reduce(w_top[:, chunks[n][0]:chunks[n][0] + 1],
                                          w_max[:, chunks[n][0]:chunks[n][0] + 1], P, RMAX).then_inc(s_wtop, 1)

            def root(n, r):
                pool.wait_ge(s_var, n + 1)
                pool.tensor_tensor(rstd[:, r:r + 1], var_scaled[:, r:r + 1], minus_half[:, :], ALU.pow)\
                    .then_inc(s_rstd, 1)

            def top_ctx(t):
                pool.wait_ge(s_ctxmax, t + 1)
                alone(pool)
                pool.partition_all_reduce(ctx_top[:, :], ctx_max[:, :], P, RMAX).then_inc(s_ctxtop, 1)

            def split_ctx(t, k):
                cols = slice(k * KC * AB // 4, (k + 1) * KC * AB // 4)
                spread = ctx_scale[:, 0:1].broadcast_to([P, KC * AB // 4])
                hi, lo = (ctx[:, s].rearrange("p c n -> p (c n)")[:, cols] for s in range(2))
                if k == 0:
                    pool.wait_ge(s_ctxscale, t + 1)
                    if not (isinstance(t, int) and t == 0):
                        pool.wait_ge(s_dense, dense0(t))
                pool.tensor_tensor(hi, ctx_in[:, cols], spread, ALU.mult).then_inc(s_ctxhi, 1)
                pool.wait_ge(s_ctxhi, 8 * t + 2 * k + 1)
                pool.tensor_tensor(ctx_in[:, cols], ctx_in[:, cols], spread, ALU.mult).then_inc(s_ctxhi, 1)
                pool.wait_ge(s_ctxhi, 8 * t + 2 * k + 2)
                pool.tensor_tensor(lo, ctx_in[:, cols], hi, ALU.subtract).then_inc(s_ctx, 1)

            def iteration(t, before=(), after=()):
                if not (isinstance(t, int) and t == NB):
                    top_ctx(t)
                    for k in range(4):
                        split_ctx(t, k)
                for n in before:
                    top(n)
                for u in range(U):
                    root(2 * t + 2 + u, u)
                for n in after:
                    top(n)

            pool.memset(ident[:, :], 0.0).then_inc(s_ident, 1)
            pool.wait_ge(s_ident, 1)
            pool.affine_select(out=ident[:, :], in_=ident[:, :], compare_op=ALU.not_equal, fill=1.0, base=0,
                               pattern=[[-1, P]], channel_multiplier=1).then_inc(s_ident, 1)
            pool.memset(v_aug, 0.0).then_inc(s_vinit, 1)
            pool.memset(minus_half[:, :], -0.5).then_inc(s_vinit, 1)
            pool.wait_ge(s_vinit, 2)
            pool.memset(v_aug[:, 0, :, :, DH:DH + 1], 1.0).then_inc(s_vinit, 1)
            for u in range(U):
                root(u, u)
            for n in range(5):
                top(n)
            top_ctx(0)
            for k in range(4):
                top(5 + k)
                split_ctx(0, k)
            top(CH_V)
            for u in range(U):
                root(2 + u, u)
            iteration(1, [CH_O], range(CH_O + 1, CH_12))
            with pool.Fori(2, NB - 1) as t:
                iteration(t)
            iteration(NB - 1, [CH_12], range(CH_12 + 1, CH_12 + 3))
            pool.wait_ge(s_bmax, 1)
            pool.partition_all_reduce(bound[:, 2:3], bound[:, 1:2], P, RMAX).then_inc(s_btop, 1)
            iteration(NB, range(CH_12 + 3, CH_3 - 1), [CH_3 - 1])
            pool.wait_ge(s_b3, 16)

            def ffn_block(f, prefetch):
                for u in range(FT):
                    if isinstance(f, int) and f == 0:
                        top(CH_3 + u)
                    if prefetch:
                        root(2 * NB + FT * (f + 1) + u, u % 2)
                pool.wait_ge(s_yres, 16 * f + 16)
                for u in range(FT):
                    ins = pool.tensor_tensor(y_res[:, u], y_res[:, u], b3_all, ALU.add)
                ins.then_inc(s_yresb, 1)

            ffn_block(0, True)
            with pool.Fori(1, NF - 1) as f:
                ffn_block(f, True)
            ffn_block(NF - 1, False)

        @block.scalar
        def _(act):
            w12_free = {CH_12: GROUPS, CH_12 + 4: GROUPS + 1, CH_12 + 5: GROUPS + 2, CH_12 + 6: GROUPS + 4}

            def high(n):
                c, _, _, _, hi, _ = chunks[n]
                act.wait_ge(s_wscale, n + 1)
                if n in w12_free:
                    act.wait_ge(s_dense, dense0(NB - 1) + w12_free[n])
                if n == CH_3:
                    act.wait_ge(s_dense, dense0(NB) + 4)
                act.activation(hi, stage(n).rearrange("p (c o) -> p c o", c=KC), ACT.Copy,
                               scale=w_scale[:, c:c + 1]).then_inc(s_whi, 1)

            def turned_hi(t):
                for q in range(4):
                    u, h = q // 2, q % 2
                    act.wait_ge(s_xt, 4 * t + q + 1)
                    if q == 0 and isinstance(t, int) and t == NB:
                        for r in range(2):
                            act.wait_ge(s_qst[r], 16 * NDMA_STACK * 2 * NB)
                        act.wait_ge(s_kst, 16 * NDMA_STACK * NB)
                    if q == 0 and not (isinstance(t, int) and t in (0, NB + 1)):
                        act.wait_ge(s_dense, dense0(t - 1) + GROUPS)
                    act.activation(rows_dst(t)[:, 0, 4 * h:4 * h + 4, P * u:P * u + P],
                                   B_XT[q][:, :].rearrange("p (c n) -> p c n", c=4), ACT.Copy).then_inc(s_xthi, 1)

            def q_hi(t, m):
                if m % 2 == 0:
                    if not (isinstance(t, int) and t == 0 and m < 4):
                        act.wait_ge(s_qst[(m // 2) % 2], 16 * NDMA_STACK * (2 * t + m // 4))
                act.wait_ge(s_dense, dense0(t) + m + 1)
                act.activation(q_part[:, (m // 2) % 2, 0, m % 2], B_DENSE[m % 2][:, 0:AB], ACT.Copy,
                               scale=Q_FACTOR).then_inc(s_dhi, 1)

            def k_hi(t, b):
                if b == 0 and not (isinstance(t, int) and t == 0):
                    act.wait_ge(s_kst, 16 * NDMA_STACK * t)
                act.wait_ge(s_dense, dense0(t) + GROUPS + b + 1)
                act.activation(k_part[:, 0, b], B_DENSE[b][:, 0:AB], ACT.Copy, scale=KV_FACTOR).then_inc(s_dhi, 1)

            def v_hi(t, u, attend):
                if u == 0 and attend:
                    act.wait_ge(s_av, 8 * t)
                act.wait_ge(s_dense, dense0(t) + GROUPS + 2 + u + 1)
                act.activation(v_aug[:, 0, u, :, 0:DH], B_DENSE[u][:, 0:KV].rearrange("p (g w) -> p g w", g=GROUPS),
                               ACT.Copy, scale=KV_FACTOR).then_inc(s_dhi, 1)

            def exps(a, m, u):
                act.wait_ge(s_neg, 8 * a + m + 1)
                for j in range(HPG):
                    s = score[:, m % 4, u, SEQ * j:SEQ * j + SEQ]
                    ins = act.activation(s, s, ACT.Exp, bias=neg_max[:, m % 4, HPG * u + j:HPG * u + j + 1],
                                         scale=c_score[:, m:m + 1])
                ins.then_inc(s_prob, 1)

            def prob_hi(a, m):
                for u in range(U):
                    if u == 0 and m >= 2:
                        act.wait_ge(s_av, 8 * a + m - 1)
                    act.wait_ge(s_pt, 16 * a + 2 * m + u + 1)
                    act.activation(prob_t[:, m % 2, 0, u], B_TURN[u][:, :], ACT.Copy).then_inc(s_pthi, 1)

            def attn_hi(t, m):
                a = t - 1
                act.wait_ge(s_ot, 8 * a + m + 1)
                if m == 0:
                    act.wait_ge(s_dense, dense0(t))
                act.activation(attn_t[:, 0, m], B_ATTN_T[:, 0:AB], ACT.Copy).then_inc(s_othi, 1)

            def iteration(t, project, attend, split=NO_SPLIT):
                a = t - 1
                first, count, at_step, at_end = split
                for s in range(STEPS):
                    if attend and 1 <= s <= GROUPS:
                        exps(a, s - 1, 0)
                    if attend and 2 <= s < GROUPS + 2:
                        prob_hi(a, s - 2)
                    if attend and 4 <= s:
                        attn_hi(t, s - 4)
                    if project and 1 <= s <= GROUPS:
                        q_hi(t, s - 1)
                    if attend and 1 <= s <= GROUPS:
                        exps(a, s - 1, 1)
                    if project and s in (GROUPS + 1, GROUPS + 2):
                        k_hi(t, s - GROUPS - 1)
                    if at_step.get(s):
                        high(first + at_step[s] - 1)
                if project:
                    v_hi(t, 0, attend)
                    v_hi(t, 1, attend)
                turned_hi(t + 1)
                for i in at_end:
                    high(first + i - 1)

            high(0)
            turned_hi(0)
            for m in range(GROUPS + 1):
                high(m + 1)
                if m:
                    q_hi(0, m - 1)
            for b in range(2):
                k_hi(0, b)
            act.wait_ge(s_vinit, 3)
            for u in range(U):
                v_hi(0, u, False)
            turned_hi(1)
            iteration(1, True, True, split=W_OUT_AT)
            with act.Fori(2, NB - 1) as t:
                iteration(t, True, True)
            iteration(NB - 1, True, True, split=W12_AT)
            iteration(NB, False, True, split=W12_AT_END)

            def y_hi(f):
                for q in range(8):
                    act.wait_ge(s_yt, 8 * (f - 1) + q + 1)
                    if q == 0:
                        act.wait_ge(s_h, 16 * f)
                    act.activation(yn[:, 0, 4 * (q % 2):4 * (q % 2) + 4, P * (q // 2):P * (q // 2) + P],
                                   B_XT[q % 4][:, :].rearrange("p (c n) -> p c n", c=4), ACT.Copy).then_inc(s_ythi, 1)

            def ffn_block(f, prefetch):
                for m in range(MC):
                    if isinstance(f, int) and f == 0 and 2 <= m < 6:
                        high(CH_3 + m - 2)
                    act.wait_ge(s_h, 16 * f + 2 * m + 1)
                    if m >= 2:
                        act.wait_ge(s_gated, 8 * f + m - 1)
                    act.activation(silu[:, m % 2], B_FFN[2 * (m % 2)][:, :], ACT.Silu, bias=b12[:, m:m + 1],
                                   scale=c_hid[:, m:m + 1]).then_inc(s_silu, 1)
                    act.wait_ge(s_gated, 8 * f + m + 1)
                    act.activation(hid[:, 0, m], gated[:, m % 2], ACT.Copy, scale=hid_scale[:, m:m + 1]).then_inc(s_hhi, 1)
                if prefetch:
                    y_hi(f + 1)

            act.wait_ge(s_const, 1)
            act.wait_ge(s_b12, 16)
            ffn_block(0, True)
            with act.Fori(1, NF - 1) as f:
                ffn_block(f, True)
            ffn_block(NF - 1, False)

        @block.tensor
        def _(pe):
            def product(dst, lhs, rhs):
                for c in range(KC):
                    for n, (a, b) in enumerate(((0, 0), (0, 1), (1, 0))):
                        ins = pe.matmul(dst, lhs(a, c), rhs(b, c), start=(c == 0 and n == 0),
                                        stop=(c == KC - 1 and n == 2))
                return ins

            def dense(t, k, dst, lhs, rhs):
                if not (isinstance(t, int) and t == 0 and k < 2):
                    pe.wait_ge(s_dread, dense0(t) + k - 1)
                product(dst, lhs, rhs).then_inc(s_dense, 1)

            def q_proj(t, m):
                if isinstance(t, int) and t == 0:
                    pe.wait_ge(s_wready, CH_Q + m + 1)
                if m == 0:
                    pe.wait_ge(s_xn, 4 * t + 4)
                dense(t, m, B_DENSE[m % 2][:, 0:AB], lambda s, c: wq[:, s, m, c], lambda s, c: xn[:, s, c])

            def k_proj(t, b):
                if b == 0:
                    pe.wait_ge(s_ctx, 4 * t + 4)
                    if isinstance(t, int) and t == 0:
                        pe.wait_ge(s_wready, CH_K + 1)
                dense(t, GROUPS + b, B_DENSE[b][:, 0:AB], lambda s, c: wk[:, s, c, P * b:P * b + P],
                      lambda s, c: ctx[:, s, c])

            def v_proj(t, u):
                if isinstance(t, int) and t == 0:
                    pe.wait_ge(s_wready, CH_V + 1)
                dense(t, GROUPS + 2 + u, B_DENSE[u][:, 0:KV], lambda s, c: ctx[:, s, c, P * u:P * u + P],
                      lambda s, c: wv[:, s, c])

            def scores(t, m):
                a = t - 1
                if m == 0:
                    pe.wait_ge(s_kst, 16 * NDMA_STACK * t)
                    pe.wait_ge(s_xn, 4 * t + 4)
                if m % 2 == 0:
                    pe.wait_ge(s_qst[(m // 2) % 2], 16 * NDMA_STACK * (2 * a + m // 4 + 1))
                for u in range(U):
                    if m >= 1:
                        pe.wait_ge(s_sread, 16 * a + 2 * m + u - 1)
                    for j in range(HPG):
                        ins = pe.matmul(B_SCORE[u][:, SEQ * j:SEQ * j + SEQ],
                                        q_stack[0:3 * DH, m, j, SEQ * u:SEQ * u + SEQ],
                                        k_stack[0:3 * DH, m // 4, m % 4, SEQ * u:SEQ * u + SEQ], start=True, stop=True)
                    ins.then_inc(s_score, 1)

            def turn_prob(a, m):
                for u in range(U):
                    pe.wait_ge(s_prob, 16 * a + 2 * m + u + 1)
                    if m >= 1:
                        pe.wait_ge(s_ptread, 16 * a + 2 * m + u - 1)
                    for j in range(HPG):
                        ins = pe.transpose(B_TURN[u][:, SEQ * j:SEQ * j + SEQ],
                                           score[:, m % 4, u, SEQ * j:SEQ * j + SEQ], ident[:, :])
                    ins.then_inc(s_pt, 1)

            def weigh(t, m):
                a = t - 1
                if m == 0:
                    pe.wait_ge(s_dread, dense0(t))
                else:
                    pe.wait_ge(s_avread, 8 * a + m)
                pe.wait_ge(s_ptread, 16 * a + 2 * m + 2)
                for u in range(U):
                    for j in range(HPG):
                        dst = B_AV[:, VW * (HPG * u + j):VW * (HPG * u + j) + VW]
                        for n, (p, v) in enumerate(((0, 0), (0, 1), (1, 0))):
                            ins = pe.matmul(dst, prob_t[:, m % 2, p, u, SEQ * j:SEQ * j + SEQ], v_aug[:, v, u, m],
                                            start=(n == 0), stop=(n == 2))
                ins.then_inc(s_av, 1)

            def turn_attn(a, m):
                pe.wait_ge(s_avread, 8 * a + m + 1)
                if m >= 1:
                    pe.wait_ge(s_otread, 8 * a + m)
                for u in range(U):
                    ins = pe.transpose(B_ATTN_T[:, P * u:P * u + P], attn[:, m % 2, P * u:P * u + P], ident[:, :])
                ins.then_inc(s_ot, 1)

            def turn_x(t, attend):
                for q in range(4):
                    u, h = q // 2, q % 2
                    if h == 0:
                        pe.wait_ge(s_norm, 2 * t + u + 1)
                    if attend and q == 0:
                        pe.wait_ge(s_sread, 16 * (t - 1))
                    if attend and q == 2:
                        pe.wait_ge(s_ptread, 16 * (t - 1))
                    for c in range(4):
                        ins = pe.transpose(B_XT[q][:, P * c:P * c + P],
                                           x_in[:, u, P * (4 * h + c):P * (4 * h + c) + P], ident[:, :])
                    ins.then_inc(s_xt, 1)

            def out_proj(t, q, k):
                a = t - 1
                h, u = q // 2, q % 2
                if q == 0:
                    pe.wait_ge(s_otread, 8 * a + 8)
                if isinstance(t, int) and t == 1 and u == 0:
                    pe.wait_ge(s_wready, CH_O + 2 * h + 2)
                dense(t, k, B_DENSE[q % 2][:, :], lambda s, c: attn_t[:, s, c, P * u:P * u + P],
                      lambda s, c: wo[:, h, s, c])

            def iteration(t, project, attend):
                a = t - 1
                for s in range(STEPS):
                    if not project and s < 4:
                        out_proj(t - 1, s, 12 + s)
                    if attend and s < GROUPS:
                        scores(t, s)
                    if attend and 2 <= s < GROUPS + 2:
                        turn_prob(a, s - 2)
                    if attend and 3 <= s < GROUPS + 3:
                        weigh(t, s - 3)
                    if attend and 4 <= s:
                        turn_attn(a, s - 4)
                    if project:
                        if s < GROUPS:
                            q_proj(t, s)
                        elif s < GROUPS + 2:
                            k_proj(t, s - GROUPS)
                        else:
                            v_proj(t, s - GROUPS - 2)
                turn_x(t + 1, attend)
                if not (isinstance(t, int) and t == NB - 1):
                    for q in range(4):
                        out_proj(t, q, 12 + q if project else q)

            pe.wait_ge(s_ident, 2)
            turn_x(0, False)
            pe.wait_ge(s_vinit, 3)
            for s in range(GROUPS):
                q_proj(0, s)
            for b in range(2):
                k_proj(0, b)
            for u in range(U):
                v_proj(0, u)
            turn_x(1, False)
            iteration(1, True, True)
            with pe.Fori(2, NB - 1) as t:
                iteration(t, True, True)
            iteration(NB - 1, True, True)
            iteration(NB, False, True)

            def turn_y(f):
                for q in range(8):
                    u, h = q // 2, q % 2
                    if h == 0:
                        pe.wait_ge(s_norm, 2 * NB + FT * f + u + 1)
                    if q >= 4:
                        pe.wait_ge(s_yn, 8 * (f - 1) + q - 3)
                    for c in range(4):
                        ins = pe.transpose(B_XT[q % 4][:, P * c:P * c + P],
                                           y_in[:, u, P * (4 * h + c):P * (4 * h + c) + P], ident[:, :])
                    ins.then_inc(s_yt, 1)

            def ffn_block(f, prefetch):
                start = isinstance(f, int) and f == 0
                if start:
                    pe.wait_ge(s_xn, 4 * (NB + 2))
                else:
                    pe.wait_ge(s_yn, 8 * f)
                for m in range(MC):
                    if start:
                        pe.wait_ge(s_wready, CH_12 + m + 1)
                        if m == 0:
                            pe.wait_ge(s_avread, 8 * NB)
                            pe.wait_ge(s_otread, 8 * NB)
                        elif m == 1:
                            pe.wait_ge(s_dread, dense0(NB) + 4)
                    elif m == 0:
                        pe.wait_ge(s_yread, 8 * f - 2)
                    elif m == 1:
                        pe.wait_ge(s_yread, 8 * f)
                    if m >= 2:
                        pe.wait_ge(s_gated, 8 * f + m - 1)
                    for k in range(2):
                        product(B_FFN[2 * (m % 2) + k][:, :], lambda s, c: w12[:, m, s, c, P * k:P * k + P],
                                lambda s, c: yn[:, s, c]).then_inc(s_h, 1)
                if prefetch:
                    turn_y(f + 1)
                if start:
                    pe.wait_ge(s_wready, NW)
                pe.wait_ge(s_hid, 8 * f + 8)
                for q in range(8):
                    u, h = q // 2, q % 2
                    if q >= 4:
                        pe.wait_ge(s_yread, 8 * f + q - 3)
                    product(B_FFN[q % 4][:, :], lambda s, c: hid[:, s, c, P * u:P * u + P],
                            lambda s, c: w3[:, h, s, c]).then_inc(s_y, 1)

            ffn_block(0, True)
            with pe.Fori(1, NF - 1) as f:
                ffn_block(f, True)
            ffn_block(NF - 1, False)

        @block.vector
        def _(dve):
            links = [0]

            def link(ins):
                ins.then_inc(s_chain, 1)
                links[0] += 1
                dve.wait_ge(s_chain, links[0])

            def chunk_max(n):
                c, slot = chunks[n][0], chunks[n][2]
                dve.wait_ge(s_wload[slot], w_arrival[n][1])
                dve.tensor_reduce(w_max[:, c:c + 1], stage(n), AX_X, ALU.max, apply_absolute_value=True)\
                   .then_inc(s_wmax, 1)

            def chunk_scale(n):
                c = slice(chunks[n][0], chunks[n][0] + 1)
                dve.wait_ge(s_wtop, n + 1)
                link(dve.tensor_scalar(w_top[:, c], w_top[:, c], 2.0 ** -100, None, ALU.max))
                link(dve.tensor_scalar(w_exp[:, c].bitcast(U32), w_top[:, c].bitcast(U32), EXPONENT, None,
                                       ALU.bitwise_and))
                link(dve.reciprocal(w_inv[:, c], w_exp[:, c]))
                dve.tensor_scalar(w_scale[:, c], w_inv[:, c], W_SCALE, None, ALU.mult).then_inc(s_wscale, 1)

            def chunk_lo(n):
                c, _, _, _, hi, lo = chunks[n]
                dve.wait_ge(s_whi, n + 1)
                dve.scalar_tensor_tensor(out=lo, in0=stage(n).rearrange("p (c o) -> p c o", c=KC),
                                         scalar=w_scale[:, c:c + 1], in1=hi,
                                         op0=ALU.mult, op1=ALU.subtract).then_inc(s_wready, 1)

            def row_stats(row_tile, n, r):
                for h in range(2):
                    ins = dve.bn_stats(stats[:, h, :], row_tile[:, HALF * h:HALF * h + HALF])
                ins.then_inc(s_stat, 1)
                dve.wait_ge(s_stat, 2 * n + 1)
                alone(dve)
                dve.bn_aggr(moments[:, r], stats[:, :, :].rearrange("p a b -> p (a b)")).then_inc(s_stat, 1)
                dve.wait_ge(s_stat, 2 * n + 2)
                dve.tensor_scalar(var_scaled[:, r:r + 1], moments[:, r, 1:2], EPS,
                                  XN_SCALE ** -2, ALU.add, ALU.mult).then_inc(s_var, 1)

            def normalise(row_tile, n, r):
                dve.wait_ge(s_rstd, n + 1)
                dve.tensor_scalar(row_tile, row_tile, moments[:, r, 0:1], rstd[:, r:r + 1],
                                  ALU.subtract, ALU.mult).then_inc(s_norm, 1)

            def turned_lo(t):
                for q in range(4):
                    u, h = q // 2, q % 2
                    dve.wait_ge(s_xthi, 4 * t + q + 1)
                    dst = (slice(None), slice(4 * h, 4 * h + 4), slice(P * u, P * u + P))
                    dve.tensor_tensor(rows_dst(t)[:, 1][dst], B_XT[q][:, :].rearrange("p (c n) -> p c n", c=4),
                                      rows_dst(t)[:, 0][dst], ALU.subtract).then_inc(s_xn, 1)

            def low(dst, src, factor, hi, n_hi):
                dve.wait_ge(s_dhi, n_hi)
                dve.scalar_tensor_tensor(out=dst, in0=src, scalar=factor, in1=hi, op0=ALU.mult, op1=ALU.subtract)\
                   .then_inc(s_dread, 1)

            def q_lo(t, m):
                low(q_part[:, (m // 2) % 2, 1, m % 2], B_DENSE[m % 2][:, 0:AB], Q_FACTOR,
                    q_part[:, (m // 2) % 2, 0, m % 2], 12 * t + m + 1)

            def k_lo(t, b):
                low(k_part[:, 1, b], B_DENSE[b][:, 0:AB], KV_FACTOR, k_part[:, 0, b], 12 * t + GROUPS + b + 1)

            def v_lo(t, u):
                low(v_aug[:, 1, u, :, 0:DH], B_DENSE[u][:, 0:KV].rearrange("p (g w) -> p g w", g=GROUPS), KV_FACTOR,
                    v_aug[:, 0, u, :, 0:DH], 12 * t + GROUPS + 2 + u + 1)

            def row_maxima(a, m):
                for u in range(U):
                    if u == 0 and m >= 4:
                        dve.wait_ge(s_pt, 16 * a + 2 * m - 6)
                    dve.wait_ge(s_score, 16 * a + 2 * m + u + 1)
                    alone(dve)
                    for j in range(HPG):
                        ins = dve.tensor_tensor_reduce(
                            score[:, m % 4, u, SEQ * j:SEQ * j + SEQ], B_SCORE[u][:, SEQ * j:SEQ * j + SEQ],
                            mask_add[:, :], 1.0, MASKED * 2, ALU.add, ALU.max,
                            row_max[:, m % 4, HPG * u + j:HPG * u + j + 1])
                    ins.then_inc(s_sread, 1)
                dve.wait_ge(s_sread, 16 * a + 2 * m + 2)
                dve.tensor_scalar(neg_max[:, m % 4, :], row_max[:, m % 4, :], c_neg[:, m:m + 1], None, ALU.mult)\
                   .then_inc(s_neg, 1)

            def prob_lo(a, m):
                for u in range(U):
                    dve.wait_ge(s_pthi, 16 * a + 2 * m + u + 1)
                    dve.tensor_tensor(prob_t[:, m % 2, 1, u], B_TURN[u][:, :], prob_t[:, m % 2, 0, u], ALU.subtract)\
                       .then_inc(s_ptread, 1)

            def divide(a, m):
                av = B_AV[:, 0:VW * U * HPG].rearrange("p (h w) -> p h w", w=VW)
                dve.wait_ge(s_av, 8 * a + m + 1)
                dve.reciprocal(inv_sum[:, :].rearrange("p (h o) -> p h o", o=1), av[:, :, DH:DH + 1]).then_inc(s_inv, 1)
                dve.wait_ge(s_inv, 8 * a + m + 1)
                if m >= 2:
                    dve.wait_ge(s_ot, 8 * a + m - 1)
                dve.tensor_tensor(attn[:, m % 2, :].rearrange("p (h w) -> p h w", w=DH), av[:, :, 0:DH],
                                  inv_sum[:, :].rearrange("p (h o) -> p h o", o=1).broadcast_to([P, U * HPG, DH]),
                                  ALU.mult).then_inc(s_avread, 1)

            def attn_lo(a, m):
                dve.wait_ge(s_othi, 8 * a + m + 1)
                dve.tensor_tensor(attn_t[:, 1, m], B_ATTN_T[:, 0:AB], attn_t[:, 0, m], ALU.subtract).then_inc(s_otread, 1)

            def ffn_factors():
                e12 = w_exp[:, CH_12:CH_12 + MC]
                link(dve.tensor_scalar(c_hid[:, :], e12, C_HID, None, ALU.mult))
                link(dve.reciprocal(c_hid_inv[:, :], c_hid[:, :]))
                link(dve.tensor_tensor(b2_scaled[:, :], b12[:, MC:2 * MC], c_hid_inv[:, :], ALU.mult))
                link(dve.tensor_reduce(bound[:, 0:1], e12, AX_X, ALU.max))
                link(dve.tensor_scalar(bound[:, 7:8], bound[:, 0:1], 2.0 ** 11, None, ALU.mult))
                dve.wait_ge(s_btop, 1)
                link(dve.tensor_tensor(bound[:, 3:4], bound[:, 7:8], bound[:, 2:3], ALU.add))
                link(dve.tensor_tensor(bound[:, 4:5], bound[:, 3:4], bound[:, 3:4], ALU.mult))
                link(dve.tensor_scalar(bound[:, 5:6].bitcast(U32), bound[:, 4:5].bitcast(U32), EXPONENT, None,
                                       ALU.bitwise_and))
                link(dve.reciprocal(bound[:, 6:7], bound[:, 5:6]))
                dve.tensor_scalar(hid_scale[:, :], c_hid[:, :], bound[:, 6:7], W_SCALE, ALU.mult, ALU.mult)\
                   .then_inc(s_const, 1)

            def output_scales(t):
                dve.tensor_scalar(c_out[:, :], out_base[:, :], ctx_exp_kept[:, 0:1], None, ALU.mult)\
                   .then_inc(s_cout, 1)
                dve.wait_ge(s_cout, t)

            def residual(t, q, k):
                h, u = q // 2, q % 2
                if q == 0:
                    dve.wait_ge(s_xres, 16 * t)
                dve.wait_ge(s_dense, dense0(t) + k + 1)
                for n in range(2):
                    cols = x_res[:, u, HALF * h + 256 * n:HALF * h + 256 * n + 256]
                    ins = dve.scalar_tensor_tensor(out=cols, in0=B_DENSE[q % 2][:, 256 * n:256 * n + 256],
                                                   scalar=c_out[:, 2 * h + n:2 * h + n + 1], in1=cols,
                                                   op0=ALU.mult, op1=ALU.add)
                ins.then_inc(s_dread, 1)

            def block_scales(t):
                if isinstance(t, int) and t == NB:
                    dve.wait_ge(s_prob, 16 * (t - 1))
                else:
                    dve.wait_ge(s_dread, dense0(t))
                dve.tensor_scalar(c_score[:, :], score_base[:, :], ctx_exp[:, 0:1], None, ALU.mult)
                dve.tensor_scalar(c_neg[:, :], score_base[:, :], ctx_exp[:, 0:1], -1.0, ALU.mult, ALU.mult)
                dve.tensor_scalar(ctx_exp_kept[:, :], ctx_exp[:, :], 1.0, None, ALU.mult).then_inc(s_scales, 1)
                dve.wait_ge(s_scales, t)

            def ctx_max_of(t):
                dve.wait_ge(s_ctxload, 16 * t + 16)
                dve.tensor_reduce(ctx_max[:, :], ctx_in[:, :], AX_X, ALU.max, apply_absolute_value=True)\
                   .then_inc(s_ctxmax, 1)

            def ctx_scale_of(t):
                dve.wait_ge(s_ctxtop, t + 1)
                dve.tensor_scalar(ctx_top[:, :], ctx_top[:, :], 2.0 ** -100, None, ALU.max).then_inc(s_ctxstep, 1)
                dve.wait_ge(s_ctxstep, 3 * t + 1)
                dve.tensor_scalar(ctx_exp[:, :].bitcast(U32), ctx_top[:, :].bitcast(U32), EXPONENT, None,
                                  ALU.bitwise_and).then_inc(s_ctxstep, 1)
                dve.wait_ge(s_ctxstep, 3 * t + 2)
                dve.reciprocal(ctx_inv[:, :], ctx_exp[:, :]).then_inc(s_ctxstep, 1)
                dve.wait_ge(s_ctxstep, 3 * t + 3)
                dve.tensor_scalar(ctx_scale[:, :], ctx_inv[:, :], W_SCALE, None, ALU.mult).then_inc(s_ctxscale, 1)

            def position_scale(split, i):
                first, count, _, _ = split
                if i:
                    chunk_scale(first + i - 1)

            def position_split(split, i):
                first, count, _, _ = split
                if i:
                    chunk_lo(first + i - 1)
                if i is not None and i < count:
                    chunk_max(first + i)

            def iteration(t, project, attend, split=NO_SPLIT):
                a = t - 1
                at_step, at_end = split[2:]
                if not project:
                    output_scales(t - 1)
                if attend:
                    block_scales(t)
                for s in range(STEPS):
                    i = at_step.get(s)
                    if attend and s < GROUPS:
                        row_maxima(a, s)
                    if project and s == 1:
                        ctx_max_of(t)
                    if project and s == 2:
                        ctx_scale_of(t)
                    if not project and s < 4:
                        residual(t - 1, s, 12 + s)
                    if attend and 2 <= s < GROUPS + 2:
                        prob_lo(a, s - 2)
                    if attend and 3 <= s < GROUPS + 3:
                        divide(a, s - 3)
                    if attend and 4 <= s:
                        attn_lo(a, s - 4)
                    position_scale(split, i)
                    if project and 1 <= s <= GROUPS:
                        q_lo(t, s - 1)
                    if s in (GROUPS, GROUPS + 1):
                        if s == GROUPS:
                            dve.wait_ge(s_xload, 16 * t + 32)
                        row_stats(x_in[:, s - GROUPS], 2 * t + 2 + s - GROUPS, s - GROUPS)
                    if s in (GROUPS + 1, GROUPS + 2):
                        normalise(x_in[:, s - GROUPS - 1], 2 * t + 1 + s - GROUPS, s - GROUPS - 1)
                    if project and s in (GROUPS + 1, GROUPS + 2):
                        k_lo(t, s - GROUPS - 1)
                    position_split(split, i)
                if project:
                    v_lo(t, 0)
                    v_lo(t, 1)
                turned_lo(t + 1)
                for i in at_end:
                    position_scale(split, i)
                    position_split(split, i)
                if isinstance(t, int) and t == 1:
                    link(dve.tensor_scalar(out_base[:, :], w_exp[:, CH_O:CH_O + 4], w_exp[:, CH_V:CH_V + 1], C_OUT,
                                           ALU.mult, ALU.mult))
                if not project:
                    ffn_factors()
                if not (isinstance(t, int) and t == NB - 1):
                    output_scales(t)
                    for q in range(4):
                        residual(t, q, 12 + q if project else q)

            dve.wait_ge(s_xload, 16)
            for u in range(U):
                row_stats(x_in[:, u], u, u)
            for u in range(U):
                normalise(x_in[:, u], u, u)
            chunk_max(0)
            chunk_max(1)
            chunk_scale(0)
            turned_lo(0)
            for m in range(GROUPS + 2):
                if m + 2 < CH_O:
                    chunk_max(m + 2)
                if m == 2:
                    ctx_max_of(0)
                if m + 1 < CH_O:
                    chunk_scale(m + 1)
                if m == 3:
                    ctx_scale_of(0)
                if m >= 2:
                    q_lo(0, m - 2)
                chunk_lo(m)
            dve.wait_ge(s_xload, 32)
            for u in range(U):
                row_stats(x_in[:, u], 2 + u, u)
            for u in range(U):
                normalise(x_in[:, u], 2 + u, u)
            link(dve.tensor_scalar(score_base[:, :], w_exp[:, CH_Q:CH_Q + GROUPS], w_exp[:, CH_K:CH_K + 1], C_SCORE,
                                   ALU.mult, ALU.mult))
            dve.wait_ge(s_mask, 16)
            link(dve.tensor_scalar(mask_add[:, :], mask_u8[:, :], -1.0, -MASKED, ALU.add, ALU.mult))
            for b in range(2):
                k_lo(0, b)
            for u in range(U):
                v_lo(0, u)
            turned_lo(1)
            iteration(1, True, True, split=W_OUT_AT)
            with dve.Fori(2, NB - 1) as t:
                iteration(t, True, True)
            iteration(NB - 1, True, True, split=W12_AT)
            dve.wait_ge(s_b12, 16)
            dve.tensor_reduce(bound[:, 1:2], b12[:, :], AX_X, ALU.max, apply_absolute_value=True).then_inc(s_bmax, 1)
            iteration(NB, False, True, split=W12_AT_END)

            def y_stats(f, u):
                if u == 0:
                    dve.wait_ge(s_yload, 16 * f)
                row_stats(y_in[:, u], 2 * NB + FT * f + u, u % 2)

            def y_norm(f, u):
                normalise(y_in[:, u], 2 * NB + FT * f + u, u % 2)

            def y_lo(f):
                for q in range(8):
                    dve.wait_ge(s_ythi, 8 * (f - 1) + q + 1)
                    dst = (slice(None), slice(4 * (q % 2), 4 * (q % 2) + 4), slice(P * (q // 2), P * (q // 2) + P))
                    dve.tensor_tensor(yn[:, 1][dst], B_XT[q % 4][:, :].rearrange("p (c n) -> p c n", c=4),
                                      yn[:, 0][dst], ALU.subtract).then_inc(s_yn, 1)

            def ffn_block(f, prefetch):
                start = isinstance(f, int) and f == 0
                for m in range(MC):
                    if start and 2 <= m < 6:
                        chunk_scale(CH_3 + m - 2)
                    dve.wait_ge(s_h, 16 * f + 2 * m + 2)
                    dve.wait_ge(s_silu, 8 * f + m + 1)
                    dve.scalar_tensor_tensor(out=gated[:, m % 2], in0=B_FFN[2 * (m % 2) + 1][:, :],
                                             scalar=b2_scaled[:, m:m + 1], in1=silu[:, m % 2], op0=ALU.add,
                                             op1=ALU.mult).then_inc(s_gated, 1)
                    dve.wait_ge(s_hhi, 8 * f + m + 1)
                    dve.scalar_tensor_tensor(out=hid[:, 1, m], in0=gated[:, m % 2], scalar=hid_scale[:, m:m + 1],
                                             in1=hid[:, 0, m], op0=ALU.mult, op1=ALU.subtract).then_inc(s_hid, 1)
                    if start and 2 <= m < 6:
                        chunk_lo(CH_3 + m - 2)
                    if prefetch and 2 <= m < 2 + FT:
                        y_stats(f + 1, m - 2)
                    if prefetch and 3 <= m < 3 + FT:
                        y_norm(f + 1, m - 3)
                    if start and 1 <= m < 5:
                        chunk_max(CH_3 + m - 1)
                if start:
                    dve.tensor_scalar(c_ffn[:, :], w_exp[:, CH_3:CH_3 + 4], bound[:, 5:6], C_FFN, ALU.mult, ALU.mult)\
                       .then_inc(s_const3, 1)
                    dve.wait_ge(s_const3, 1)
                if prefetch:
                    y_lo(f + 1)
                dve.wait_ge(s_yresb, f + 1)
                for q in range(8):
                    u, h = q // 2, q % 2
                    dve.wait_ge(s_y, 8 * f + q + 1)
                    for k in range(2):
                        cols = y_res[:, u, HALF * h + 256 * k:HALF * h + 256 * k + 256]
                        ins = dve.scalar_tensor_tensor(out=cols, in0=B_FFN[q % 4][:, 256 * k:256 * k + 256],
                                                       scalar=c_ffn[:, 2 * h + k:2 * h + k + 1], in1=cols,
                                                       op0=ALU.mult, op1=ALU.add)
                    ins.then_inc(s_yread, 1)

            ffn_block(0, True)
            with dve.Fori(1, NF - 1) as f:
                ffn_block(f, True)
            ffn_block(NF - 1, False)


_OUT = (16, 128, 1024)


def kernel(x, ctx_4096, mask_SxS2_bk0, L0_xattn_w_q, L0_xattn_w_k, L0_xattn_w_v, L0_xattn_w_out, L0_ffn_w12,
           L0_ffn_b12, L0_ffn_w3, L0_ffn_b3):
    import numpy as np
    import concourse.bacc as bacc
    from concourse.bass_utils import run_bass_kernel_spmd

    def cols(w, n):
        w = np.asarray(w)
        return np.ascontiguousarray(w.reshape(w.shape[0] // n, n, KC, P).transpose(0, 3, 2, 1))\
            .reshape(w.shape[0] // n, P, KC * n)

    w12 = np.asarray(L0_ffn_w12).reshape(2, MC, P, D).transpose(1, 0, 2, 3).reshape(2 * M, D)
    ctx = np.asarray(ctx_4096).reshape(NB, AB, KC, P).transpose(0, 3, 2, 1)
    arrays = {
        "x": np.ascontiguousarray(np.asarray(x).reshape(TOK, D)),
        "ctx_t": np.ascontiguousarray(ctx).reshape(NB, P, KC * AB),
        "mask": np.ascontiguousarray(mask_SxS2_bk0),
        "wq_t": cols(L0_xattn_w_q, P),
        "wk_t": cols(L0_xattn_w_k, KV)[0],
        "wv_t": cols(L0_xattn_w_v, KV)[0],
        "wo_t": cols(L0_xattn_w_out, 256),
        "w12_t": cols(w12, 2 * P),
        "b12_t": np.ascontiguousarray(np.asarray(L0_ffn_b12).reshape(2 * MC, P).T),
        "w3_t": cols(L0_ffn_w3, 256),
        "b3_row": np.ascontiguousarray(np.asarray(L0_ffn_b3).reshape(1, D)),
    }
    nc = bacc.Bacc("TRN2", target_bir_lowering=False, num_devices=1)
    args = [nc.dram_tensor(name, a.shape, mybir.dt.from_np(a.dtype), kind="ExternalInput").ap()
            for name, a in arrays.items()]
    out = nc.dram_tensor("out", (TOK, D), F32, kind="ExternalOutput").ap()
    xattn_ffn(nc, *args, out)
    r = run_bass_kernel_spmd(nc, [arrays], core_ids=[0])
    return r.results[0]["out"].reshape(_OUT)
```

```python
from contextlib import ExitStack

import concourse.bass as bass
from concourse import mybir

F32 = mybir.dt.float32
F16 = mybir.dt.float16
BF16 = mybir.dt.bfloat16
U32 = mybir.dt.uint32
U8 = mybir.dt.uint8
ALU = mybir.AluOpType
ACT = mybir.ActivationFunctionType
AX_X = mybir.AxisListType.X
RMAX = bass.bass_isa.ReduceOp.max

P = 128
D = 1024
KC = D // P
SEQ = 128
HEADS, GROUPS, DH = 32, 8, 32
HPG = HEADS // GROUPS
KV = GROUPS * DH
TOK = 16 * SEQ
U = 2
AB = U * SEQ
NB = TOK // AB
FB = 512
NF = TOK // FB
FT = FB // P
M = D
MC = M // P
HALF = 512
EPS = 1e-5
VW = DH + 2
EXPONENT = 0x7F800000
MASKED = -(2.0 ** 100)
XN_SCALE = 2.0 ** 8
W_SCALE = 2.0 ** 13
Q_FACTOR = 2.0 ** -13 * DH ** -0.5
KV_FACTOR = 2.0 ** -20
C_SCORE = 2.0 ** -14
C_OUT = 2.0 ** -19
C_HID = 2.0 ** -21
C_FFN = 2.0 ** -26
NDMA_STACK = 12


def xattn_ffn(nc, x, ctx_t, mask, wq_t, wk_t, wv_t, wo_t, w12_t, b12_t, w3_t, b3_row, out):
    x_blocks = x.rearrange("(b u p) d -> b p u d", b=NB, p=P)
    x1_dram = nc.dram_tensor("x1_scratch", (TOK, D), F32, kind="Internal").ap()
    x1_blocks = x1_dram.rearrange("(b u p) d -> b p u d", b=NB, p=P)
    x1_ffn = x1_dram.rearrange("(b u p) d -> b p u d", b=NF, p=P)
    out_ffn = out.rearrange("(b u p) d -> b p u d", b=NF, p=P)

    def at(blocks, i):
        return blocks[bass.ds(i, 1)].rearrange("o p u d -> (o p) u d")

    with ExitStack() as stack:
        def sb(name, shape, dt):
            return stack.enter_context(nc.sbuf_tensor(name, shape, dt))

        def sem(name):
            return stack.enter_context(nc.semaphore(name))

        arena_in = sb("arena_in", [P, 32768], F16)
        arena_out = sb("arena_out", [P, 16384], F16)
        arena_work = sb("arena_work", [P, 32768], F16)
        wstage = sb("wstage", [P, 4096], F32)

        def carve(arena, at_, n, dt=F16):
            w = n * (2 if dt is F32 else 1)
            v = arena[:, at_:at_ + w]
            return (v.bitcast(dt) if dt is F32 else v), at_ + w

        o = 0
        wq, o = carve(arena_in, o, 2 * GROUPS * KC * P)
        wq = wq.rearrange("p (s m c o) -> p s m c o", s=2, m=GROUPS, c=KC)
        ctx_in, o = carve(arena_in, o, KC * AB, F32)
        wk, o = carve(arena_in, o, 2 * KC * KV)
        wk = wk.rearrange("p (s c o) -> p s c o", s=2, c=KC)
        wv, o = carve(arena_in, o, 2 * KC * KV)
        wv = wv.rearrange("p (s c o) -> p s c o", s=2, c=KC)
        ctx, o = carve(arena_in, o, 2 * KC * AB)
        ctx = ctx.rearrange("p (s c n) -> p s c n", s=2, c=KC)
        wo = arena_out[:, :].rearrange("p (h s c o) -> p h s c o", h=2, s=2, c=KC)
        w12 = arena_in[:, :].rearrange("p (m s c o) -> p m s c o", m=MC, s=2, c=KC)
        w3 = wo

        o = 0
        x_in, o = carve(arena_work, o, U * D, F32)
        x_in = x_in.rearrange("p (u d) -> p u d", u=U)
        x_res, o = carve(arena_work, o, U * D, F32)
        x_res = x_res.rearrange("p (u d) -> p u d", u=U)
        xn, o = carve(arena_work, o, 2 * KC * AB)
        xn = xn.rearrange("p (s c n) -> p s c n", s=2, c=KC)
        q_part, o = carve(arena_work, o, 2 * 2 * 4 * AB)
        q_part = q_part.rearrange("p (r s g n) -> p r s g n", r=2, s=2, g=4)
        assert o <= 2 * FT * D + 2 * KC * FB, o
        o = 2 * FT * D + 2 * KC * FB
        q_stack, o = carve(arena_work, o, HEADS * AB)
        q_stack = q_stack.rearrange("p (g j n) -> p g j n", g=GROUPS, j=HPG)
        k_stack, o = carve(arena_work, o, GROUPS * AB)
        k_stack = k_stack.rearrange("p (b g n) -> p b g n", b=2, g=GROUPS // 2)
        v_aug, o = carve(arena_work, o, 2 * U * GROUPS * VW)
        v_aug = v_aug.rearrange("p (s u g w) -> p s u g w", s=2, u=U, g=GROUPS)
        attn_t, o = carve(arena_work, o, 2 * GROUPS * AB)
        attn_t = attn_t.rearrange("p (s g n) -> p s g n", s=2, g=GROUPS)
        assert o <= arena_work.shape[1], o
        score = sb("score", [P, 4, U, HPG * SEQ], F32)
        prob_t = sb("prob_t", [P, 2, 2, U, HPG * SEQ], F16)
        attn = sb("attn", [P, 2, U * HPG * DH], F32)
        k_part = sb("k_part", [P, 2, 2, AB], F16)

        o = 0
        y_in, o = carve(arena_work, o, FT * D, F32)
        y_in = y_in.rearrange("p (u d) -> p u d", u=FT)
        yn, o = carve(arena_work, o, 2 * KC * FB)
        yn = yn.rearrange("p (s c n) -> p s c n", s=2, c=KC)
        hid, o = carve(arena_work, o, 2 * MC * FB)
        hid = hid.rearrange("p (s c n) -> p s c n", s=2, c=MC)
        y_res, o = carve(arena_work, o, FT * D, F32)
        y_res = y_res.rearrange("p (u d) -> p u d", u=FT)
        assert o <= arena_work.shape[1], o
        silu = prob_t[:, :, :, :, :].rearrange("p a b c d -> p (a b c d)")[:, 0:2 * 2 * FB].bitcast(F32) \
            .rearrange("p (r n) -> p r n", r=2)
        gated = score[:, 0, :, :]
        b3_all = score[:, 2, :, :].rearrange("p u n -> p (u n)")

        ident = sb("ident", [P, P], F32)
        mask_u8 = sb("mask_u8", [P, SEQ], U8)
        mask_add = sb("mask_add", [P, SEQ], F32)
        b12 = sb("b12", [P, 2 * MC], F32)
        b2_scaled = sb("b2_scaled", [P, MC], F32)
        NW = GROUPS + 2 + 4 + MC + 4
        NSCALE = NW - (MC - 1)
        CH_Q, CH_K, CH_V, CH_O = 0, GROUPS, GROUPS + 1, GROUPS + 2
        CH_12, CH_3 = CH_O + 4, CH_O + 4 + MC
        w_max = sb("w_max", [P, NSCALE], F32)
        w_top = sb("w_top", [P, NSCALE], F32)
        w_exp = sb("w_exp", [P, NSCALE], F32)
        w_inv = sb("w_inv", [P, NSCALE], F32)
        w_scale = sb("w_scale", [P, NSCALE], F32)
        ctx_max = sb("ctx_max", [P, 1], F32)
        ctx_top = sb("ctx_top", [P, 1], F32)
        ctx_exp = sb("ctx_exp", [P, 1], F32)
        ctx_inv = sb("ctx_inv", [P, 1], F32)
        ctx_scale = sb("ctx_scale", [P, 1], F32)
        score_base = sb("score_base", [P, GROUPS], F32)
        out_base = sb("out_base", [P, 4], F32)
        c_score = sb("c_score", [P, GROUPS], F32)
        c_neg = sb("c_neg", [P, GROUPS], F32)
        c_out = sb("c_out", [P, 4], F32)
        ctx_exp_kept = sb("ctx_exp_kept", [P, 1], F32)
        w12_part = sb("w12_part", [P, 1], F32)
        c_hid = sb("c_hid", [P, 1], F32)
        c_hid_inv = sb("c_hid_inv", [P, 1], F32)
        hid_scale = sb("hid_scale", [P, 1], F32)
        c_ffn = sb("c_ffn", [P, 4], F32)
        bound = sb("bound", [P, 8], F32)
        row_max = sb("row_max", [P, 4, U * HPG], F32)
        neg_max = sb("neg_max", [P, 4, U * HPG], F32)
        inv_sum = sb("inv_sum", [P, U * HPG], F32)
        stats = sb("stats", [P, 2, 6], F32)
        moments = sb("moments", [P, 2, 2], F32)
        var_scaled = sb("var_scaled", [P, 2], F32)
        rstd = sb("rstd", [P, 2], F32)
        minus_half = sb("minus_half", [P, 1], F32)

        bank = [stack.enter_context(nc.psum_tensor(f"bank{i}", [P, HALF], F32)) for i in range(8)]
        B_SCORE, B_TURN, B_AV, B_ATTN_T, B_DENSE = bank[0:2], bank[2:4], bank[4], bank[5], bank[6:8]
        B_FFN = bank[4:8]
        B_XT = bank[0:4]

        s_mask, s_b12, s_b3 = sem("mask_loaded"), sem("b12_loaded"), sem("b3_loaded")
        s_wload = [sem(f"weights_loaded_{i}") for i in range(8)]
        s_wload += [sem(f"weights_loaded_{i}") if i in (11, 14, 15) else None for i in range(8, 16)]
        s_wlook, s_w12max, s_w12init = sem("w12_looked_at"), sem("w12_max_step"), sem("w12_max_init")
        s_wmax, s_wtop, s_wscale = sem("w_max_done"), sem("w_top_done"), sem("w_scale_done")
        s_whi, s_wready = sem("w_hi_done"), sem("w_ready")
        s_wscaled, s_wpool = sem("w_scaled_on_pool"), sem("w_ready_on_pool")
        s_ident, s_vinit = sem("ident_done"), sem("v_init_done")
        s_xfirst = sem("first_row_tile_loaded")
        s_xload, s_ctxload, s_xres = sem("x_loaded"), sem("ctx_loaded"), sem("x_res_loaded")
        s_ctxmax, s_ctxtop, s_ctxscale = sem("ctx_max_done"), sem("ctx_top_done"), sem("ctx_scale_done")
        s_ctxhi, s_ctx = sem("ctx_hi_done"), sem("ctx_ready")
        s_norm, s_stat, s_var, s_rstd = sem("norm_done"), sem("stats_done"), sem("var_done"), sem("rstd_done")
        s_xt, s_xthi, s_xn = sem("x_turned"), sem("xn_hi_done"), sem("xn_ready")
        s_dense, s_dhi, s_dread = sem("dense_done"), sem("dense_hi_done"), sem("dense_read")
        s_qst = [sem("q_stack_loaded_0"), sem("q_stack_loaded_1")]
        s_kst = sem("k_stack_loaded")
        s_score, s_sread, s_neg, s_prob = sem("score_done"), sem("score_read"), sem("neg_max_done"), sem("prob_done")
        s_pt, s_pthi, s_ptread = sem("prob_turned"), sem("prob_t_hi_done"), sem("prob_t_ready")
        s_av, s_inv, s_avread = sem("av_done"), sem("inv_sum_done"), sem("attn_ready")
        s_ot, s_othi, s_otread = sem("attn_turned"), sem("attn_t_hi_done"), sem("attn_t_ready")
        s_cout, s_x1 = sem("c_out_done"), sem("x1_stored")
        s_chain, s_alone = sem("vector_chain"), sem("waits_alone")
        s_const, s_const3 = sem("ffn_consts_done"), sem("ffn_out_consts_done")
        s_scales, s_ctxstep = sem("block_scales_done"), sem("ctx_step_done")
        s_bmax, s_btop = sem("b_max_done"), sem("b_top_done")
        s_yload, s_yres, s_yresb = sem("y_loaded"), sem("y_res_loaded"), sem("y_res_with_b3")
        s_yt, s_ythi, s_yn = sem("y_turned"), sem("yn_hi_done"), sem("yn_ready")
        s_h, s_silu, s_gated = sem("h_done"), sem("silu_done"), sem("gated_done")
        s_hhi, s_hid = sem("hid_hi_done"), sem("hid_ready")
        s_y, s_yread, s_out = sem("y_done"), sem("ffn_bank_read"), sem("out_stored")

        block = stack.enter_context(nc.Block())

        def dense0(t):
            return 0 if isinstance(t, int) and t == 0 else 16 * t - 4

        STEPS = GROUPS + 4
        CTX_SCALE_AT = 1
        ROWS_AT, ROWS_AT_END = GROUPS, 6

        def alone(engine):
            engine.sem_inc(s_alone, 1)

        chunks = []
        for m in range(GROUPS):
            chunks.append((CH_Q + m, wq_t[m], m, 1, wq[:, 0, m], wq[:, 1, m]))
        chunks.append((CH_K, wk_t, 0, 2, wk[:, 0], wk[:, 1]))
        chunks.append((CH_V, wv_t, 2, 2, wv[:, 0], wv[:, 1]))
        for k in range(4):
            quarter = [wo[:, k // 2, part, :, 256 * (k % 2):256 * (k % 2) + 256] for part in range(2)]
            chunks.append((CH_O + k, wo_t[k], 2 * (k % 2), 2, quarter[0], quarter[1]))
        for m in range(MC):
            slot = (0, 2, 8 + 3, 0, 2, 8 + 6, 8 + 7, 0)[m]
            chunks.append((CH_12 + m, w12_t[m], slot, 2 if slot < 8 else 1, w12[:, m, 0], w12[:, m, 1]))
        for k in range(4):
            quarter = [w3[:, k // 2, part, :, 256 * (k % 2):256 * (k % 2) + 256] for part in range(2)]
            chunks.append((CH_3 + k, w3_t[k], 2 * (k % 2), 2, quarter[0], quarter[1]))
        last_user, w_arrival, loads = [None] * 16, [], [0] * 16
        for n, (_, _, slot, width, _, _) in enumerate(chunks):
            free_after = [last_user[s] for s in range(slot, slot + width) if last_user[s] is not None]
            for s in range(slot, slot + width):
                last_user[s] = n
            loads[slot] += 16
            w_arrival.append((free_after, loads[slot]))

        def stage(n):
            _, _, slot, width, _, _ = chunks[n]
            if slot >= 8:
                return arena_in[:, 4096 * (slot - 8):4096 * (slot - 7)].bitcast(F32)
            if slot >= 4:
                return score[:, slot - 4, :, :].rearrange("p u n -> p (u n)")
            return wstage[:, slot * 1024:(slot + width) * 1024]

        def scale_of(n):
            return n if n <= CH_12 else CH_12 if n < CH_3 else n - (MC - 1)

        def col(n):
            return slice(scale_of(n), scale_of(n) + 1)

        W_OUT_AT = {GROUPS: CH_O + 1, GROUPS + 2: CH_O + 2, STEPS: CH_O + 3}
        W_OUT_SUM_AT = {GROUPS + 1: CH_O + 2, GROUPS + 3: CH_O + 3}
        W12_AT = {GROUPS + 1: CH_12, GROUPS + 2: CH_12 + 1, STEPS: CH_12 + 2}
        W12_ON_POOL = (CH_12 + 2, CH_12 + 4, CH_12 + 6)
        W12_AT_END = {0: CH_12 + 3, 1: CH_12 + 4, 2: CH_12 + 5, 3: CH_12 + 6, STEPS: CH_12 + 7}

        def ready(n):
            if n in W12_ON_POOL:
                return s_wpool, W12_ON_POOL.index(n) + 1
            return s_wready, sum(k not in W12_ON_POOL for k in range(n + 1))

        def split_in(t):
            if isinstance(t, int) and t == 1:
                return W_OUT_AT
            if isinstance(t, int) and t == NB - 1:
                return W12_AT
            if isinstance(t, int) and t == NB:
                return W12_AT_END
            return {}

        def rows_dst(t):
            if isinstance(t, int) and t >= NB:
                return yn[:, :, :, AB * (t - NB):AB * (t - NB) + AB]
            return xn

        @block.sync
        def _(sp):
            def load_chunk(n):
                for last in sorted(set(w_arrival[n][0])):
                    sp.wait_ge(*ready(last))
                if n == CH_12 + 2:
                    sp.wait_ge(s_dense, dense0(NB - 1) + GROUPS)
                if n in (CH_12 + 5, CH_12 + 6):
                    sp.wait_ge(s_dense, dense0(NB - 1) + GROUPS + 4)
                sp.dma_start(stage(n), chunks[n][1]).then_inc(s_wload[chunks[n][2]], 16)

            def load_ctx(t):
                sp.wait_ge(s_ctx, 4 * t)
                alone(sp)
                sp.dma_start(ctx_in[:, :], ctx_t[bass.ds(t, 1)].rearrange("o p n -> (o p) n")).then_inc(s_ctxload, 16)

            def stack_q(t, half):
                sp.wait_ge(s_dread, dense0(t) + 4 * half + 4)
                for j in range(HPG):
                    for r, part in ((0, 0), (1, 1), (2, 0)):
                        sp.dma_start(q_stack[DH * r:DH * r + DH, 4 * half:4 * half + 4, j, :],
                                     q_part[DH * j:DH * j + DH, half, part]).then_inc(s_qst[half], 16)

            def stack_k(t):
                sp.wait_ge(s_dread, dense0(t) + GROUPS + 2)
                for g in range(4):
                    for r, part in ((0, 0), (1, 0), (2, 1)):
                        sp.dma_start(k_stack[DH * r:DH * r + DH, :, g, :],
                                     k_part[DH * g:DH * g + DH, part]).then_inc(s_kst, 16)

            def load_x(t):
                sp.wait_ge(s_xt, 4 * t)
                alone(sp)
                rows = at(x1_blocks, t - NB) if isinstance(t, int) and t >= NB else at(x_blocks, t)
                sp.dma_start(x_in, rows).then_inc(s_xload, 16)

            def store_x1(t):
                sp.wait_ge(s_dread, dense0(t + 1) if not (isinstance(t, int) and t == NB) else dense0(t) + 4)
                alone(sp)
                sp.dma_start(at(x1_blocks, t - 1), x_res).then_inc(s_x1, 16)
                if not (isinstance(t, int) and t == NB):
                    sp.wait_ge(s_x1, 16 * t)
                    alone(sp)
                    sp.dma_start(x_res, at(x_blocks, t)).then_inc(s_xres, 16)

            def iteration(t, early=(), late=(), tail=()):
                load_x(t + 1)
                for n in early:
                    load_chunk(n)
                for half in range(2):
                    sp.wait_ge(s_score, 16 * (t - 1) + 8 * half + 8)
                    alone(sp)
                    stack_q(t, half)
                    if half == 0 and not (isinstance(t, int) and t == NB - 1):
                        load_ctx(t + 1)
                for n in late:
                    load_chunk(n)
                sp.wait_ge(s_score, 16 * t)
                alone(sp)
                stack_k(t)
                for n in tail:
                    load_chunk(n)

            sp.dma_start(x_in[:, 0], x_blocks[0, :, 0]).then_inc(s_xfirst, 16)
            sp.dma_start(x_in[:, 1], x_blocks[0, :, 1]).then_inc(s_xload, 16)
            load_chunk(0)
            load_chunk(1)
            sp.dma_start(mask_u8[:, :], mask).then_inc(s_mask, 16)
            load_chunk(2)
            load_chunk(3)
            sp.dma_start(ctx_in[:, :], ctx_t[0]).then_inc(s_ctxload, 16)
            for n in range(4, GROUPS):
                load_chunk(n)
            load_x(1)
            load_chunk(CH_K)
            load_chunk(CH_V)
            stack_q(0, 0)
            load_chunk(CH_O)
            load_chunk(CH_O + 1)
            stack_q(0, 1)
            stack_k(0)
            load_ctx(1)
            sp.dma_start(x_res, at(x_blocks, 0)).then_inc(s_xres, 16)
            sp.dma_start(b12[:, :], b12_t).then_inc(s_b12, 16)
            iteration(1, early=(CH_O + 2,), late=(CH_O + 3,))
            store_x1(1)
            sp.wait_ge(*ready(CH_O + 3))
            with sp.Fori(2, NB - 1) as t:
                iteration(t)
                sp.dma_start(wstage[:, :].rearrange("p (k n) -> p k n", k=2),
                             w12_t[bass.ds((2 * t) % MC, 2)].rearrange("k p n -> p k n")).then_inc(s_wlook, 16)
                store_x1(t)
                sp.wait_ge(s_w12max, 2 * t - 3)
                alone(sp)
            iteration(NB - 1, early=(CH_12, CH_12 + 1), late=(CH_12 + 2,),
                      tail=range(CH_12 + 3, CH_12 + 7))
            load_x(NB + 1)
            load_chunk(CH_12 + 7)
            store_x1(NB - 1)
            store_x1(NB)

            def ffn_block(f, prefetch):
                if prefetch:
                    if isinstance(f, int) and f == 0:
                        sp.wait_ge(s_xt, 4 * (NB + 2))
                        sp.wait_ge(s_x1, 16 * NB)
                    else:
                        sp.wait_ge(s_yt, 8 * f)
                        alone(sp)
                    sp.dma_start(y_in, at(x1_ffn, f + 1)).then_inc(s_yload, 16)
                if isinstance(f, int) and f == 0:
                    for n in range(CH_3 + 2, NW):
                        load_chunk(n)
                for u in range(FT):
                    sp.wait_ge(s_yread, 8 * f + 2 * u + 2)
                    alone(sp)
                    sp.dma_start(at(out_ffn, f)[:, u], y_res[:, u]).then_inc(s_out, 16)
                sp.wait_ge(s_out, 16 * FT * (f + 1))
                alone(sp)
                if prefetch:
                    sp.dma_start(y_res, at(x1_ffn, f + 1)).then_inc(s_yres, 16)

            load_chunk(CH_3)
            load_chunk(CH_3 + 1)
            sp.wait_ge(s_pt, 16 * NB)
            sp.dma_start(b3_all, b3_row.broadcast_to([P, D])).then_inc(s_b3, 16)
            sp.wait_ge(s_dense, dense0(NB) + 4)
            sp.dma_start(y_res, at(x1_ffn, 0)).then_inc(s_yres, 16)
            ffn_block(0, True)
            with sp.Fori(1, NF - 1) as f:
                ffn_block(f, True)
            ffn_block(NF - 1, False)

        @block.gpsimd
        def _(pool):
            def top(n):
                pool.wait_ge(s_wmax, scale_of(n) + 1)
                pool.partition_all_reduce(w_top[:, col(n)], w_max[:, col(n)], P, RMAX).then_inc(s_wtop, 1)

            def chunk_lo(n):
                _, _, _, _, hi, lo = chunks[n]
                i = W12_ON_POOL.index(n)
                src = stage(n)
                pool.wait_ge(s_whi, n + 1)
                pool.tensor_tensor(src, src, w_scale[:, col(n)].broadcast_to([P, src.shape[1]]), ALU.mult)\
                    .then_inc(s_wscaled, 1)
                pool.wait_ge(s_wscaled, i + 1)
                pool.tensor_tensor(lo, src.rearrange("p (c o) -> p c o", c=KC), hi, ALU.subtract)\
                    .then_inc(s_wpool, 1)

            def root(n, r):
                pool.wait_ge(s_var, n + 1)
                pool.tensor_tensor(rstd[:, r:r + 1], var_scaled[:, r:r + 1], minus_half[:, :], ALU.pow)\
                    .then_inc(s_rstd, 1)

            def top_ctx(t):
                pool.wait_ge(s_ctxmax, t + 1)
                alone(pool)
                pool.partition_all_reduce(ctx_top[:, :], ctx_max[:, :], P, RMAX).then_inc(s_ctxtop, 1)

            def split_ctx(t, k):
                cols = slice(k * KC * AB // 4, (k + 1) * KC * AB // 4)
                spread = ctx_scale[:, 0:1].broadcast_to([P, KC * AB // 4])
                hi, lo = (ctx[:, s].rearrange("p c n -> p (c n)")[:, cols] for s in range(2))
                if k == 0:
                    pool.wait_ge(s_ctxscale, t + 1)
                    if not (isinstance(t, int) and t == 0):
                        pool.wait_ge(s_dense, dense0(t))
                pool.tensor_tensor(hi, ctx_in[:, cols], spread, ALU.mult).then_inc(s_ctxhi, 1)
                pool.wait_ge(s_ctxhi, 8 * t + 2 * k + 1)
                pool.tensor_tensor(ctx_in[:, cols], ctx_in[:, cols], spread, ALU.mult).then_inc(s_ctxhi, 1)
                pool.wait_ge(s_ctxhi, 8 * t + 2 * k + 2)
                pool.tensor_tensor(lo, ctx_in[:, cols], hi, ALU.subtract).then_inc(s_ctx, 1)

            def iteration(t, tops=(), tops_after=(), los=(), los_after=()):
                if not (isinstance(t, int) and t == NB):
                    top_ctx(t)
                    for k in range(4):
                        split_ctx(t, k)
                for n in tops:
                    top(n)
                for n in los:
                    chunk_lo(n)
                for u in range(U):
                    root(2 * t + 2 + u, u)
                for n in tops_after:
                    top(n)
                for n in los_after:
                    chunk_lo(n)

            pool.memset(ident[:, :], 0.0).then_inc(s_ident, 1)
            pool.wait_ge(s_ident, 1)
            pool.affine_select(out=ident[:, :], in_=ident[:, :], compare_op=ALU.not_equal, fill=1.0, base=0,
                               pattern=[[-1, P]], channel_multiplier=1).then_inc(s_ident, 1)
            pool.memset(v_aug, 0.0).then_inc(s_vinit, 1)
            pool.memset(minus_half[:, :], -0.5).then_inc(s_vinit, 1)
            pool.memset(w_max[:, col(CH_12)], 0.0).then_inc(s_w12init, 1)
            pool.wait_ge(s_vinit, 2)
            pool.memset(v_aug[:, 0, :, :, DH:DH + 1], 1.0).then_inc(s_vinit, 1)
            for u in range(U):
                root(u, u)
            for n in range(5):
                top(n)
            top_ctx(0)
            for k in range(4):
                top(5 + k)
                split_ctx(0, k)
                if k >= 2:
                    root(k, k - 2)
            for n in range(CH_V, CH_O + 2):
                top(n)
            iteration(1, tops_after=range(CH_O + 2, CH_12))
            with pool.Fori(2, NB - 1) as t:
                iteration(t)
            iteration(NB - 1, tops=[CH_12], los_after=W12_ON_POOL[:1])
            pool.wait_ge(s_bmax, 1)
            pool.partition_all_reduce(bound[:, 2:3], bound[:, 1:2], P, RMAX).then_inc(s_btop, 1)
            iteration(NB, los=W12_ON_POOL[1:])
            pool.wait_ge(s_b3, 16)

            def ffn_block(f, prefetch):
                for u in range(FT):
                    if isinstance(f, int) and f == 0:
                        top(CH_3 + u)
                    if prefetch:
                        root(2 * NB + FT * (f + 1) + u, u % 2)
                pool.wait_ge(s_yres, 16 * f + 16)
                for u in range(FT):
                    ins = pool.tensor_tensor(y_res[:, u], y_res[:, u], b3_all, ALU.add)
                ins.then_inc(s_yresb, 1)

            ffn_block(0, True)
            with pool.Fori(1, NF - 1) as f:
                ffn_block(f, True)
            ffn_block(NF - 1, False)

        @block.scalar
        def _(act):
            w12_free = {CH_12: GROUPS, CH_12 + 4: GROUPS + 1, CH_12 + 5: GROUPS + 2, CH_12 + 6: GROUPS + 4}

            def high(n):
                _, _, slot, _, hi, _ = chunks[n]
                act.wait_ge(s_wload[slot], w_arrival[n][1])
                act.wait_ge(s_wscale, scale_of(n) + 1)
                if n in (CH_12 + 3, CH_12 + 6, CH_12 + 7):
                    act.wait_ge(*ready(n - 1))
                if n in w12_free:
                    act.wait_ge(s_dense, dense0(NB - 1) + w12_free[n])
                if n == CH_3:
                    act.wait_ge(s_dense, dense0(NB) + 4)
                act.activation(hi, stage(n).rearrange("p (c o) -> p c o", c=KC), ACT.Copy,
                               scale=w_scale[:, col(n)]).then_inc(s_whi, 1)

            def chunk_sum(n):
                _, _, slot, _, hi, _ = chunks[n]
                act.wait_ge(s_wload[slot], w_arrival[n][1])
                act.activation(hi.bitcast(BF16), stage(n).rearrange("p (c o) -> p c o", c=KC), ACT.Abs,
                               accum_out=w_max[:, col(n)]).then_inc(s_wmax, 1)

            def turned_hi(t):
                for q in range(4):
                    u, h = q // 2, q % 2
                    act.wait_ge(s_xt, 4 * t + q + 1)
                    if q == 0 and isinstance(t, int) and t == NB:
                        for r in range(2):
                            act.wait_ge(s_qst[r], 16 * NDMA_STACK * NB)
                    if q == 0 and not (isinstance(t, int) and t in (0, NB + 1)):
                        act.wait_ge(s_dense, dense0(t - 1) + GROUPS)
                    act.activation(rows_dst(t)[:, 0, 4 * h:4 * h + 4, P * u:P * u + P],
                                   B_XT[q][:, :].rearrange("p (c n) -> p c n", c=4), ACT.Copy).then_inc(s_xthi, 1)

            def q_hi(t, m):
                if m % 4 == 0 and not (isinstance(t, int) and t == 0):
                    act.wait_ge(s_qst[m // 4], 16 * NDMA_STACK * t)
                act.wait_ge(s_dense, dense0(t) + m + 1)
                act.activation(q_part[:, m // 4, 0, m % 4], B_DENSE[m % 2][:, 0:AB], ACT.Copy,
                               scale=Q_FACTOR).then_inc(s_dhi, 1)

            def k_hi(t, b):
                if b == 0 and not (isinstance(t, int) and t == 0):
                    act.wait_ge(s_kst, 16 * NDMA_STACK * t)
                act.wait_ge(s_dense, dense0(t) + GROUPS + b + 1)
                act.activation(k_part[:, 0, b], B_DENSE[b][:, 0:AB], ACT.Copy, scale=KV_FACTOR).then_inc(s_dhi, 1)

            def v_hi(t, u, attend):
                if u == 0 and attend:
                    act.wait_ge(s_av, 8 * t)
                act.wait_ge(s_dense, dense0(t) + GROUPS + 2 + u + 1)
                act.activation(v_aug[:, 0, u, :, 0:DH], B_DENSE[u][:, 0:KV].rearrange("p (g w) -> p g w", g=GROUPS),
                               ACT.Copy, scale=KV_FACTOR).then_inc(s_dhi, 1)

            def exps(a, m, u):
                act.wait_ge(s_neg, 8 * a + m + 1)
                for j in range(HPG):
                    s = score[:, m % 4, u, SEQ * j:SEQ * j + SEQ]
                    ins = act.activation(s, s, ACT.Exp, bias=neg_max[:, m % 4, HPG * u + j:HPG * u + j + 1],
                                         scale=c_score[:, m:m + 1])
                ins.then_inc(s_prob, 1)

            def prob_hi(a, m):
                for u in range(U):
                    if u == 0 and m >= 2:
                        act.wait_ge(s_av, 8 * a + m - 1)
                    act.wait_ge(s_pt, 16 * a + 2 * m + u + 1)
                    act.activation(prob_t[:, m % 2, 0, u], B_TURN[u][:, :], ACT.Copy).then_inc(s_pthi, 1)

            def attn_hi(t, m):
                a = t - 1
                act.wait_ge(s_ot, 8 * a + m + 1)
                if m == 0:
                    act.wait_ge(s_dense, dense0(t))
                act.activation(attn_t[:, 0, m], B_ATTN_T[:, 0:AB], ACT.Copy).then_inc(s_othi, 1)

            def iteration(t, project, attend):
                a = t - 1
                split = split_in(t)
                for s in range(STEPS):
                    if attend and 1 <= s <= GROUPS:
                        exps(a, s - 1, 0)
                    if attend and 2 <= s < GROUPS + 2:
                        prob_hi(a, s - 2)
                    if s in split:
                        high(split[s])
                    if attend and 4 <= s:
                        attn_hi(t, s - 4)
                    if project and 1 <= s <= GROUPS:
                        q_hi(t, s - 1)
                    if attend and 1 <= s <= GROUPS:
                        exps(a, s - 1, 1)
                    if project and s in (GROUPS + 1, GROUPS + 2):
                        k_hi(t, s - GROUPS - 1)
                    if isinstance(t, int) and t == 1 and s in W_OUT_SUM_AT:
                        chunk_sum(W_OUT_SUM_AT[s])
                if project:
                    v_hi(t, 0, attend)
                    v_hi(t, 1, attend)
                turned_hi(t + 1)
                if STEPS in split:
                    high(split[STEPS])

            chunk_sum(0)
            chunk_sum(1)
            high(0)
            turned_hi(0)
            for m in range(GROUPS + 2):
                if m + 2 < CH_O:
                    chunk_sum(m + 2)
                if m + 1 < CH_O:
                    high(m + 1)
                if 1 <= m <= GROUPS:
                    q_hi(0, m - 1)
            turned_hi(1)
            chunk_sum(CH_O)
            k_hi(0, 0)
            high(CH_O)
            k_hi(0, 1)
            chunk_sum(CH_O + 1)
            act.wait_ge(s_vinit, 3)
            for u in range(U):
                v_hi(0, u, False)
            iteration(1, True, True)
            with act.Fori(2, NB - 1) as t:
                iteration(t, True, True)
            iteration(NB - 1, True, True)
            iteration(NB, False, True)

            def y_hi(f):
                for q in range(8):
                    act.wait_ge(s_yt, 8 * (f - 1) + q + 1)
                    if q == 0:
                        act.wait_ge(s_h, 16 * f)
                    act.activation(yn[:, 0, 4 * (q % 2):4 * (q % 2) + 4, P * (q // 2):P * (q // 2) + P],
                                   B_XT[q % 4][:, :].rearrange("p (c n) -> p c n", c=4), ACT.Copy).then_inc(s_ythi, 1)

            def ffn_block(f, prefetch):
                for m in range(MC):
                    if isinstance(f, int) and f == 0 and 2 <= m < 6:
                        high(CH_3 + m - 2)
                    act.wait_ge(s_h, 16 * f + 2 * m + 1)
                    if m >= 2:
                        act.wait_ge(s_gated, 8 * f + m - 1)
                    act.activation(silu[:, m % 2], B_FFN[2 * (m % 2)][:, :], ACT.Silu, bias=b12[:, m:m + 1],
                                   scale=c_hid[:, 0:1]).then_inc(s_silu, 1)
                    act.wait_ge(s_gated, 8 * f + m + 1)
                    act.activation(hid[:, 0, m], gated[:, m % 2], ACT.Copy, scale=hid_scale[:, 0:1])\
                       .then_inc(s_hhi, 1)
                if prefetch:
                    y_hi(f + 1)

            act.wait_ge(s_const, 1)
            act.wait_ge(s_b12, 16)
            ffn_block(0, True)
            with act.Fori(1, NF - 1) as f:
                ffn_block(f, True)
            ffn_block(NF - 1, False)

        @block.tensor
        def _(pe):
            def product(dst, lhs, rhs, before=None):
                for c in range(KC):
                    if before:
                        before(c)
                    for n, (a, b) in enumerate(((0, 0), (0, 1), (1, 0))):
                        ins = pe.matmul(dst, lhs(a, c), rhs(b, c), start=(c == 0 and n == 0),
                                        stop=(c == KC - 1 and n == 2))
                return ins

            def dense(t, k, dst, lhs, rhs):
                if not (isinstance(t, int) and t == 0 and k < 2):
                    pe.wait_ge(s_dread, dense0(t) + k - 1)
                product(dst, lhs, rhs).then_inc(s_dense, 1)

            def q_proj(t, m):
                if isinstance(t, int) and t == 0:
                    pe.wait_ge(*ready(CH_Q + m))
                if m == 0:
                    pe.wait_ge(s_xn, 4 * t + 4)
                dense(t, m, B_DENSE[m % 2][:, 0:AB], lambda s, c: wq[:, s, m, c], lambda s, c: xn[:, s, c])

            def k_proj(t, b):
                if b == 0:
                    pe.wait_ge(s_ctx, 4 * t + 4)
                    if isinstance(t, int) and t == 0:
                        pe.wait_ge(*ready(CH_K))
                dense(t, GROUPS + b, B_DENSE[b][:, 0:AB], lambda s, c: wk[:, s, c, P * b:P * b + P],
                      lambda s, c: ctx[:, s, c])

            def v_proj(t, u):
                if isinstance(t, int) and t == 0:
                    pe.wait_ge(*ready(CH_V))
                dense(t, GROUPS + 2 + u, B_DENSE[u][:, 0:KV], lambda s, c: ctx[:, s, c, P * u:P * u + P],
                      lambda s, c: wv[:, s, c])

            def scores(t, m):
                a = t - 1
                if m == 0:
                    pe.wait_ge(s_kst, 16 * NDMA_STACK * t)
                    pe.wait_ge(s_xn, 4 * t + 4)
                if m % 4 == 0:
                    pe.wait_ge(s_qst[m // 4], 16 * NDMA_STACK * t)
                for u in range(U):
                    if m >= 1:
                        pe.wait_ge(s_sread, 16 * a + 2 * m + u - 1)
                    for j in range(HPG):
                        ins = pe.matmul(B_SCORE[u][:, SEQ * j:SEQ * j + SEQ],
                                        q_stack[0:3 * DH, m, j, SEQ * u:SEQ * u + SEQ],
                                        k_stack[0:3 * DH, m // 4, m % 4, SEQ * u:SEQ * u + SEQ],
                                        start=True, stop=True)
                    ins.then_inc(s_score, 1)

            def turn_prob(a, m):
                for u in range(U):
                    pe.wait_ge(s_prob, 16 * a + 2 * m + u + 1)
                    if m >= 1:
                        pe.wait_ge(s_ptread, 16 * a + 2 * m + u - 1)
                    for j in range(HPG):
                        ins = pe.transpose(B_TURN[u][:, SEQ * j:SEQ * j + SEQ],
                                           score[:, m % 4, u, SEQ * j:SEQ * j + SEQ], ident[:, :])
                    ins.then_inc(s_pt, 1)

            def weigh(t, m):
                a = t - 1
                if m == 0:
                    pe.wait_ge(s_dread, dense0(t))
                else:
                    pe.wait_ge(s_avread, 8 * a + m)
                pe.wait_ge(s_ptread, 16 * a + 2 * m + 2)
                for u in range(U):
                    for j in range(HPG):
                        dst = B_AV[:, VW * (HPG * u + j):VW * (HPG * u + j) + VW]
                        for n, (p, v) in enumerate(((0, 0), (0, 1), (1, 0))):
                            ins = pe.matmul(dst, prob_t[:, m % 2, p, u, SEQ * j:SEQ * j + SEQ], v_aug[:, v, u, m],
                                            start=(n == 0), stop=(n == 2))
                ins.then_inc(s_av, 1)

            def turn_attn(a, m):
                pe.wait_ge(s_avread, 8 * a + m + 1)
                if m >= 1:
                    pe.wait_ge(s_otread, 8 * a + m)
                for u in range(U):
                    ins = pe.transpose(B_ATTN_T[:, P * u:P * u + P], attn[:, m % 2, P * u:P * u + P], ident[:, :])
                ins.then_inc(s_ot, 1)

            def turn_x(t, attend):
                for q in range(4):
                    u, h = q // 2, q % 2
                    if h == 0:
                        pe.wait_ge(s_norm, 2 * t + u + 1)
                    if attend and q == 0:
                        pe.wait_ge(s_sread, 16 * (t - 1))
                    if attend and q == 2:
                        pe.wait_ge(s_ptread, 16 * (t - 1))
                    for c in range(4):
                        ins = pe.transpose(B_XT[q][:, P * c:P * c + P],
                                           x_in[:, u, P * (4 * h + c):P * (4 * h + c) + P], ident[:, :])
                    ins.then_inc(s_xt, 1)

            def out_proj(t, q, k):
                a = t - 1
                h, u = q // 2, q % 2
                if q == 0:
                    pe.wait_ge(s_otread, 8 * a + 8)
                if isinstance(t, int) and t == 1 and u == 0:
                    pe.wait_ge(*ready(CH_O + 2 * h + 1))
                dense(t, k, B_DENSE[q % 2][:, :], lambda s, c: attn_t[:, s, c, P * u:P * u + P],
                      lambda s, c: wo[:, h, s, c])

            def iteration(t, project, attend):
                a = t - 1
                for s in range(STEPS):
                    if not project and s < 4:
                        out_proj(t - 1, s, 12 + s)
                    if attend and s < GROUPS:
                        scores(t, s)
                    if attend and 2 <= s < GROUPS + 2:
                        turn_prob(a, s - 2)
                    if attend and 3 <= s < GROUPS + 3:
                        weigh(t, s - 3)
                    if attend and 4 <= s:
                        turn_attn(a, s - 4)
                    if project:
                        if s < GROUPS:
                            q_proj(t, s)
                        elif s < GROUPS + 2:
                            k_proj(t, s - GROUPS)
                        else:
                            v_proj(t, s - GROUPS - 2)
                turn_x(t + 1, attend)
                if not (isinstance(t, int) and t == NB - 1):
                    for q in range(4):
                        out_proj(t, q, 12 + q if project else q)

            pe.wait_ge(s_ident, 2)
            turn_x(0, False)
            pe.wait_ge(s_vinit, 3)
            for s in range(GROUPS):
                q_proj(0, s)
            turn_x(1, False)
            for b in range(2):
                k_proj(0, b)
            for u in range(U):
                v_proj(0, u)
            iteration(1, True, True)
            with pe.Fori(2, NB - 1) as t:
                iteration(t, True, True)
            iteration(NB - 1, True, True)
            iteration(NB, False, True)

            def turn_y(f, half):
                for q in range(4 * half, 4 * half + 4):
                    u, h = q // 2, q % 2
                    if h == 0:
                        pe.wait_ge(s_norm, 2 * NB + FT * f + u + 1)
                    if q >= 4:
                        pe.wait_ge(s_yn, 8 * (f - 1) + q - 3)
                    for c in range(4):
                        ins = pe.transpose(B_XT[q % 4][:, P * c:P * c + P],
                                           y_in[:, u, P * (4 * h + c):P * (4 * h + c) + P], ident[:, :])
                    ins.then_inc(s_yt, 1)

            def ffn_block(f, prefetch):
                start = isinstance(f, int) and f == 0
                if start:
                    pe.wait_ge(s_xn, 4 * (NB + 2))
                else:
                    pe.wait_ge(s_yn, 8 * f)
                for m in range(MC):
                    if start:
                        pe.wait_ge(*ready(CH_12 + m))
                        if m == 0:
                            pe.wait_ge(s_avread, 8 * NB)
                            pe.wait_ge(s_otread, 8 * NB)
                        elif m == 1:
                            pe.wait_ge(s_dread, dense0(NB) + 4)
                    elif m == 0:
                        pe.wait_ge(s_yread, 8 * f - 2)
                    elif m == 1:
                        pe.wait_ge(s_yread, 8 * f)
                    if m >= 2:
                        pe.wait_ge(s_gated, 8 * f + m - 1)
                    for k in range(2):
                        product(B_FFN[2 * (m % 2) + k][:, :], lambda s, c: w12[:, m, s, c, P * k:P * k + P],
                                lambda s, c: yn[:, s, c]).then_inc(s_h, 1)
                if prefetch:
                    turn_y(f + 1, 0)
                if start:
                    pe.wait_ge(*ready(NW - 1))
                pe.wait_ge(s_hid, 8 * f + MC - 1)
                for q in range(8):
                    u, h = q // 2, q % 2
                    if q >= 4:
                        pe.wait_ge(s_yread, 8 * f + q - 3)

                    def last_hidden(c):
                        if q == 0 and c == KC - 1:
                            pe.wait_ge(s_hid, 8 * f + MC)
                    product(B_FFN[q % 4][:, :], lambda s, c: hid[:, s, c, P * u:P * u + P],
                            lambda s, c: w3[:, h, s, c], last_hidden).then_inc(s_y, 1)
                    if q == 0 and prefetch:
                        turn_y(f + 1, 1)

            ffn_block(0, True)
            with pe.Fori(1, NF - 1) as f:
                ffn_block(f, True)
            ffn_block(NF - 1, False)

        @block.vector
        def _(dve):
            links = [0]

            def link(ins):
                ins.then_inc(s_chain, 1)
                links[0] += 1
                dve.wait_ge(s_chain, links[0])

            def chunk_max(n):
                slot = chunks[n][2]
                dve.wait_ge(s_wload[slot], w_arrival[n][1])
                dve.tensor_reduce(w_max[:, col(n)], stage(n), AX_X, ALU.max, apply_absolute_value=True)\
                   .then_inc(s_wmax, 1)

            def chunk_scale(n):
                c = col(n)
                dve.wait_ge(s_wtop, scale_of(n) + 1)
                link(dve.tensor_scalar(w_top[:, c], w_top[:, c], 2.0 ** -100, None, ALU.max))
                link(dve.tensor_scalar(w_exp[:, c].bitcast(U32), w_top[:, c].bitcast(U32), EXPONENT, None,
                                       ALU.bitwise_and))
                link(dve.reciprocal(w_inv[:, c], w_exp[:, c]))
                dve.tensor_scalar(w_scale[:, c], w_inv[:, c], W_SCALE, None, ALU.mult).then_inc(s_wscale, 1)

            def chunk_lo(n):
                _, _, _, _, hi, lo = chunks[n]
                dve.wait_ge(s_whi, n + 1)
                dve.scalar_tensor_tensor(out=lo, in0=stage(n).rearrange("p (c o) -> p c o", c=KC),
                                         scalar=w_scale[:, col(n)], in1=hi,
                                         op0=ALU.mult, op1=ALU.subtract).then_inc(s_wready, 1)

            def row_stats(row_tile, n, r):
                for h in range(2):
                    ins = dve.bn_stats(stats[:, h, :], row_tile[:, HALF * h:HALF * h + HALF])
                ins.then_inc(s_stat, 1)
                dve.wait_ge(s_stat, 2 * n + 1)
                alone(dve)
                dve.bn_aggr(moments[:, r], stats[:, :, :].rearrange("p a b -> p (a b)")).then_inc(s_stat, 1)
                dve.wait_ge(s_stat, 2 * n + 2)
                dve.tensor_scalar(var_scaled[:, r:r + 1], moments[:, r, 1:2], EPS,
                                  XN_SCALE ** -2, ALU.add, ALU.mult).then_inc(s_var, 1)

            def normalise(row_tile, n, r):
                dve.wait_ge(s_rstd, n + 1)
                dve.tensor_scalar(row_tile, row_tile, moments[:, r, 0:1], rstd[:, r:r + 1],
                                  ALU.subtract, ALU.mult).then_inc(s_norm, 1)

            def turned_lo(t):
                for q in range(4):
                    u, h = q // 2, q % 2
                    dve.wait_ge(s_xthi, 4 * t + q + 1)
                    dst = (slice(None), slice(4 * h, 4 * h + 4), slice(P * u, P * u + P))
                    dve.tensor_tensor(rows_dst(t)[:, 1][dst], B_XT[q][:, :].rearrange("p (c n) -> p c n", c=4),
                                      rows_dst(t)[:, 0][dst], ALU.subtract).then_inc(s_xn, 1)

            def low(dst, src, factor, hi, n_hi):
                dve.wait_ge(s_dhi, n_hi)
                dve.scalar_tensor_tensor(out=dst, in0=src, scalar=factor, in1=hi, op0=ALU.mult, op1=ALU.subtract)\
                   .then_inc(s_dread, 1)

            def q_lo(t, m):
                low(q_part[:, m // 4, 1, m % 4], B_DENSE[m % 2][:, 0:AB], Q_FACTOR,
                    q_part[:, m // 4, 0, m % 4], 12 * t + m + 1)

            def k_lo(t, b):
                low(k_part[:, 1, b], B_DENSE[b][:, 0:AB], KV_FACTOR, k_part[:, 0, b], 12 * t + GROUPS + b + 1)

            def v_lo(t, u):
                low(v_aug[:, 1, u, :, 0:DH], B_DENSE[u][:, 0:KV].rearrange("p (g w) -> p g w", g=GROUPS), KV_FACTOR,
                    v_aug[:, 0, u, :, 0:DH], 12 * t + GROUPS + 2 + u + 1)

            def row_maxima(a, m):
                for u in range(U):
                    if u == 0 and m >= 4:
                        dve.wait_ge(s_pt, 16 * a + 2 * m - 6)
                    dve.wait_ge(s_score, 16 * a + 2 * m + u + 1)
                    alone(dve)
                    for j in range(HPG):
                        ins = dve.tensor_tensor_reduce(
                            score[:, m % 4, u, SEQ * j:SEQ * j + SEQ], B_SCORE[u][:, SEQ * j:SEQ * j + SEQ],
                            mask_add[:, :], 1.0, MASKED * 2, ALU.add, ALU.max,
                            row_max[:, m % 4, HPG * u + j:HPG * u + j + 1])
                    ins.then_inc(s_sread, 1)
                dve.wait_ge(s_sread, 16 * a + 2 * m + 2)
                dve.tensor_scalar(neg_max[:, m % 4, :], row_max[:, m % 4, :], c_neg[:, m:m + 1], None, ALU.mult)\
                   .then_inc(s_neg, 1)

            def prob_lo(a, m):
                for u in range(U):
                    dve.wait_ge(s_pthi, 16 * a + 2 * m + u + 1)
                    dve.tensor_tensor(prob_t[:, m % 2, 1, u], B_TURN[u][:, :], prob_t[:, m % 2, 0, u], ALU.subtract)\
                       .then_inc(s_ptread, 1)

            def divide(a, m):
                av = B_AV[:, 0:VW * U * HPG].rearrange("p (h w) -> p h w", w=VW)
                dve.wait_ge(s_av, 8 * a + m + 1)
                dve.reciprocal(inv_sum[:, :].rearrange("p (h o) -> p h o", o=1), av[:, :, DH:DH + 1])\
                   .then_inc(s_inv, 1)
                dve.wait_ge(s_inv, 8 * a + m + 1)
                if m >= 2:
                    dve.wait_ge(s_ot, 8 * a + m - 1)
                dve.tensor_tensor(attn[:, m % 2, :].rearrange("p (h w) -> p h w", w=DH), av[:, :, 0:DH],
                                  inv_sum[:, :].rearrange("p (h o) -> p h o", o=1).broadcast_to([P, U * HPG, DH]),
                                  ALU.mult).then_inc(s_avread, 1)

            def attn_lo(a, m):
                dve.wait_ge(s_othi, 8 * a + m + 1)
                dve.tensor_tensor(attn_t[:, 1, m], B_ATTN_T[:, 0:AB], attn_t[:, 0, m], ALU.subtract)\
                   .then_inc(s_otread, 1)

            def ffn_factors():
                e12 = w_exp[:, col(CH_12)]
                link(dve.tensor_scalar(c_hid[:, :], e12, C_HID, None, ALU.mult))
                link(dve.reciprocal(c_hid_inv[:, :], c_hid[:, :]))
                link(dve.tensor_tensor(b2_scaled[:, :], b12[:, MC:2 * MC], c_hid_inv[:, 0:1].broadcast_to([P, MC]),
                                       ALU.mult))
                link(dve.tensor_scalar(bound[:, 7:8], e12, 2.0 ** 11, None, ALU.mult))
                dve.wait_ge(s_btop, 1)
                link(dve.tensor_tensor(bound[:, 3:4], bound[:, 7:8], bound[:, 2:3], ALU.add))
                link(dve.tensor_tensor(bound[:, 4:5], bound[:, 3:4], bound[:, 3:4], ALU.mult))
                link(dve.tensor_scalar(bound[:, 5:6].bitcast(U32), bound[:, 4:5].bitcast(U32), EXPONENT, None,
                                       ALU.bitwise_and))
                link(dve.reciprocal(bound[:, 6:7], bound[:, 5:6]))
                dve.tensor_scalar(hid_scale[:, :], c_hid[:, :], bound[:, 6:7], W_SCALE, ALU.mult, ALU.mult)\
                   .then_inc(s_const, 1)

            def output_scales(t):
                dve.tensor_scalar(c_out[:, :], out_base[:, :], ctx_exp_kept[:, 0:1], None, ALU.mult)\
                   .then_inc(s_cout, 1)
                dve.wait_ge(s_cout, t)

            def residual(t, q, k):
                h, u = q // 2, q % 2
                if q == 0:
                    dve.wait_ge(s_xres, 16 * t)
                dve.wait_ge(s_dense, dense0(t) + k + 1)
                for n in range(2):
                    cols = x_res[:, u, HALF * h + 256 * n:HALF * h + 256 * n + 256]
                    ins = dve.scalar_tensor_tensor(out=cols, in0=B_DENSE[q % 2][:, 256 * n:256 * n + 256],
                                                   scalar=c_out[:, 2 * h + n:2 * h + n + 1], in1=cols,
                                                   op0=ALU.mult, op1=ALU.add)
                ins.then_inc(s_dread, 1)

            def block_scales(t):
                if isinstance(t, int) and t == NB:
                    dve.wait_ge(s_prob, 16 * (t - 1))
                else:
                    dve.wait_ge(s_dread, dense0(t))
                dve.tensor_scalar(c_score[:, :], score_base[:, :], ctx_exp[:, 0:1], None, ALU.mult)
                dve.tensor_scalar(c_neg[:, :], score_base[:, :], ctx_exp[:, 0:1], -1.0, ALU.mult, ALU.mult)
                dve.tensor_scalar(ctx_exp_kept[:, :], ctx_exp[:, :], 1.0, None, ALU.mult).then_inc(s_scales, 1)
                dve.wait_ge(s_scales, t)

            def ctx_max_of(t):
                dve.wait_ge(s_ctxload, 16 * t + 16)
                dve.tensor_reduce(ctx_max[:, :], ctx_in[:, :], AX_X, ALU.max, apply_absolute_value=True)\
                   .then_inc(s_ctxmax, 1)

            def ctx_scale_of(t):
                dve.wait_ge(s_ctxtop, t + 1)
                dve.tensor_scalar(ctx_top[:, :], ctx_top[:, :], 2.0 ** -100, None, ALU.max).then_inc(s_ctxstep, 1)
                dve.wait_ge(s_ctxstep, 3 * t + 1)
                dve.tensor_scalar(ctx_exp[:, :].bitcast(U32), ctx_top[:, :].bitcast(U32), EXPONENT, None,
                                  ALU.bitwise_and).then_inc(s_ctxstep, 1)
                dve.wait_ge(s_ctxstep, 3 * t + 2)
                dve.reciprocal(ctx_inv[:, :], ctx_exp[:, :]).then_inc(s_ctxstep, 1)
                dve.wait_ge(s_ctxstep, 3 * t + 3)
                dve.tensor_scalar(ctx_scale[:, :], ctx_inv[:, :], W_SCALE, None, ALU.mult).then_inc(s_ctxscale, 1)

            def look_at_w12(t):
                dve.wait_ge(s_wlook, 16 * (t - 1))
                dve.tensor_reduce(w12_part[:, :], wstage[:, :], AX_X, ALU.max, apply_absolute_value=True)\
                   .then_inc(s_w12max, 1)
                dve.wait_ge(s_w12max, 2 * t - 3)
                top12 = w_max[:, col(CH_12)]
                dve.tensor_tensor(top12, top12, w12_part[:, :], ALU.max).then_inc(s_w12max, 1)

            def iteration(t, project, attend):
                a = t - 1
                split = split_in(t)
                if isinstance(t, int) and t == NB - 1:
                    dve.wait_ge(s_w12max, 2 * (NB - 3))
                    dve.sem_inc(s_wmax, 1)
                if not project:
                    output_scales(t - 1)
                if attend:
                    block_scales(t)
                for s in range(STEPS):
                    if attend and s < GROUPS:
                        row_maxima(a, s)
                    if s in split and split[s] < CH_12:
                        chunk_scale(split[s])
                    if s == 0 and isinstance(t, int) and t == 1:
                        ctx_max_of(t)
                    if project and s == CTX_SCALE_AT:
                        ctx_scale_of(t)
                    if not project and s < 4:
                        residual(t - 1, s, 12 + s)
                    if attend and 2 <= s < GROUPS + 2:
                        prob_lo(a, s - 2)
                    if attend and 3 <= s < GROUPS + 3:
                        divide(a, s - 3)
                    if attend and 4 <= s:
                        attn_lo(a, s - 4)
                    if project and 1 <= s <= GROUPS:
                        q_lo(t, s - 1)
                    if project and s in (GROUPS + 1, GROUPS + 2):
                        k_lo(t, s - GROUPS - 1)
                    r0 = ROWS_AT if project else ROWS_AT_END
                    if s == r0:
                        dve.wait_ge(s_xload, 16 * t + 32)
                    if s in (r0, r0 + 1):
                        row_stats(x_in[:, s - r0], 2 * t + 2 + s - r0, s - r0)
                    if s in (r0 + 1, r0 + 2):
                        normalise(x_in[:, s - r0 - 1], 2 * t + 1 + s - r0, s - r0 - 1)
                    if s in split and split[s] not in W12_ON_POOL:
                        chunk_lo(split[s])
                    if s == 5 and isinstance(t, int) and t == NB - 1:
                        chunk_scale(CH_12)
                if project:
                    v_lo(t, 0)
                    v_lo(t, 1)
                turned_lo(t + 1)
                if STEPS in split:
                    if split[STEPS] < CH_12:
                        chunk_scale(split[STEPS])
                    if split[STEPS] not in W12_ON_POOL:
                        chunk_lo(split[STEPS])
                if isinstance(t, int) and t == 1:
                    link(dve.tensor_scalar(out_base[:, :], w_exp[:, CH_O:CH_O + 4], w_exp[:, CH_V:CH_V + 1], C_OUT,
                                           ALU.mult, ALU.mult))
                if not project:
                    ffn_factors()
                if not (isinstance(t, int) and t == NB - 1):
                    output_scales(t)
                    for q in range(4):
                        residual(t, q, 12 + q if project else q)
                        if q == 0 and project:
                            ctx_max_of(t + 1)
                        if q == 1 and not isinstance(t, int):
                            look_at_w12(t)

            dve.wait_ge(s_xfirst, 16)
            row_stats(x_in[:, 0], 0, 0)
            dve.wait_ge(s_xload, 16)
            row_stats(x_in[:, 1], 1, 1)
            for u in range(U):
                normalise(x_in[:, u], u, u)
            chunk_scale(0)
            chunk_lo(0)
            turned_lo(0)
            for m in range(GROUPS + 2):
                if m == 2:
                    ctx_max_of(0)
                if m + 1 < CH_O:
                    chunk_scale(m + 1)
                if m == 3:
                    ctx_scale_of(0)
                if 2 <= m < GROUPS:
                    q_lo(0, m - 2)
                if m:
                    chunk_lo(m)
                if m >= GROUPS:
                    q_lo(0, m - 2)
                if m == 5:
                    dve.wait_ge(s_xload, 32)
                if m in (5, 6):
                    row_stats(x_in[:, m - 5], m - 3, m - 5)
                if m in (6, 7):
                    normalise(x_in[:, m - 6], m - 4, m - 6)
            turned_lo(1)
            k_lo(0, 0)
            chunk_scale(CH_O)
            k_lo(0, 1)
            chunk_lo(CH_O)
            v_lo(0, 0)
            v_lo(0, 1)
            link(dve.tensor_scalar(score_base[:, :], w_exp[:, CH_Q:CH_Q + GROUPS], w_exp[:, CH_K:CH_K + 1], C_SCORE,
                                   ALU.mult, ALU.mult))
            dve.wait_ge(s_mask, 16)
            link(dve.tensor_scalar(mask_add[:, :], mask_u8[:, :], -1.0, -MASKED, ALU.add, ALU.mult))
            iteration(1, True, True)
            dve.wait_ge(s_w12init, 1)
            with dve.Fori(2, NB - 1) as t:
                iteration(t, True, True)
            iteration(NB - 1, True, True)
            dve.wait_ge(s_b12, 16)
            dve.tensor_reduce(bound[:, 1:2], b12[:, :], AX_X, ALU.max, apply_absolute_value=True).then_inc(s_bmax, 1)
            iteration(NB, False, True)

            def y_stats(f, u):
                if u == 0:
                    dve.wait_ge(s_yload, 16 * f)
                row_stats(y_in[:, u], 2 * NB + FT * f + u, u % 2)

            def y_norm(f, u):
                normalise(y_in[:, u], 2 * NB + FT * f + u, u % 2)

            def y_lo(f):
                for q in range(8):
                    dve.wait_ge(s_ythi, 8 * (f - 1) + q + 1)
                    dst = (slice(None), slice(4 * (q % 2), 4 * (q % 2) + 4), slice(P * (q // 2), P * (q // 2) + P))
                    dve.tensor_tensor(yn[:, 1][dst], B_XT[q % 4][:, :].rearrange("p (c n) -> p c n", c=4),
                                      yn[:, 0][dst], ALU.subtract).then_inc(s_yn, 1)

            def ffn_block(f, prefetch):
                start = isinstance(f, int) and f == 0
                for m in range(MC):
                    if start and 2 <= m < 6:
                        chunk_scale(CH_3 + m - 2)
                    dve.wait_ge(s_h, 16 * f + 2 * m + 2)
                    dve.wait_ge(s_silu, 8 * f + m + 1)
                    dve.scalar_tensor_tensor(out=gated[:, m % 2], in0=B_FFN[2 * (m % 2) + 1][:, :],
                                             scalar=b2_scaled[:, m:m + 1], in1=silu[:, m % 2], op0=ALU.add,
                                             op1=ALU.mult).then_inc(s_gated, 1)
                    dve.wait_ge(s_hhi, 8 * f + m + 1)
                    dve.scalar_tensor_tensor(out=hid[:, 1, m], in0=gated[:, m % 2], scalar=hid_scale[:, 0:1],
                                             in1=hid[:, 0, m], op0=ALU.mult, op1=ALU.subtract).then_inc(s_hid, 1)
                    if start and 2 <= m < 6:
                        chunk_lo(CH_3 + m - 2)
                    if prefetch and 2 <= m < 2 + FT:
                        y_stats(f + 1, m - 2)
                    if prefetch and 3 <= m < 3 + FT:
                        y_norm(f + 1, m - 3)
                    if start and 1 <= m < 5:
                        chunk_max(CH_3 + m - 1)
                if start:
                    dve.tensor_scalar(c_ffn[:, :], w_exp[:, scale_of(CH_3):NSCALE], bound[:, 5:6], C_FFN,
                                      ALU.mult, ALU.mult).then_inc(s_const3, 1)
                    dve.wait_ge(s_const3, 1)
                if prefetch:
                    y_lo(f + 1)
                dve.wait_ge(s_yresb, f + 1)
                for q in range(8):
                    u, h = q // 2, q % 2
                    dve.wait_ge(s_y, 8 * f + q + 1)
                    for k in range(2):
                        cols = y_res[:, u, HALF * h + 256 * k:HALF * h + 256 * k + 256]
                        ins = dve.scalar_tensor_tensor(out=cols, in0=B_FFN[q % 4][:, 256 * k:256 * k + 256],
                                                       scalar=c_ffn[:, 2 * h + k:2 * h + k + 1], in1=cols,
                                                       op0=ALU.mult, op1=ALU.add)
                    ins.then_inc(s_yread, 1)

            ffn_block(0, True)
            with dve.Fori(1, NF - 1) as f:
                ffn_block(f, True)
            ffn_block(NF - 1, False)


_OUT = (16, 128, 1024)


def kernel(x, ctx_4096, mask_SxS2_bk0, L0_xattn_w_q, L0_xattn_w_k, L0_xattn_w_v, L0_xattn_w_out, L0_ffn_w12,
           L0_ffn_b12, L0_ffn_w3, L0_ffn_b3):
    import numpy as np
    import concourse.bacc as bacc
    from concourse.bass_utils import run_bass_kernel_spmd

    def cols(w, n):
        w = np.asarray(w)
        return np.ascontiguousarray(w.reshape(w.shape[0] // n, n, KC, P).transpose(0, 3, 2, 1))\
            .reshape(w.shape[0] // n, P, KC * n)

    w12 = np.asarray(L0_ffn_w12).reshape(2, MC, P, D).transpose(1, 0, 2, 3).reshape(2 * M, D)
    ctx = np.asarray(ctx_4096).reshape(NB, AB, KC, P).transpose(0, 3, 2, 1)
    arrays = {
        "x": np.ascontiguousarray(np.asarray(x).reshape(TOK, D)),
        "ctx_t": np.ascontiguousarray(ctx).reshape(NB, P, KC * AB),
        "mask": np.ascontiguousarray(mask_SxS2_bk0),
        "wq_t": cols(L0_xattn_w_q, P),
        "wk_t": cols(L0_xattn_w_k, KV)[0],
        "wv_t": cols(L0_xattn_w_v, KV)[0],
        "wo_t": cols(L0_xattn_w_out, 256),
        "w12_t": cols(w12, 2 * P),
        "b12_t": np.ascontiguousarray(np.asarray(L0_ffn_b12).reshape(2 * MC, P).T),
        "w3_t": cols(L0_ffn_w3, 256),
        "b3_row": np.ascontiguousarray(np.asarray(L0_ffn_b3).reshape(1, D)),
    }
    nc = bacc.Bacc("TRN2", target_bir_lowering=False, num_devices=1)
    args = [nc.dram_tensor(name, a.shape, mybir.dt.from_np(a.dtype), kind="ExternalInput").ap()
            for name, a in arrays.items()]
    out = nc.dram_tensor("out", (TOK, D), F32, kind="ExternalOutput").ap()
    xattn_ffn(nc, *args, out)
    r = run_bass_kernel_spmd(nc, [arrays], core_ids=[0])
    return r.results[0]["out"].reshape(_OUT)
```
